# Optimizing a Trainium2 kernel written in Bass

```python
import numpy as np
import jax
import jax.numpy as jnp

def _softmax(x, axis=-1):
    return jax.nn.softmax(x, axis=axis)

def _gelu(x):
    return jax.nn.gelu(x, approximate=True)

def _silu(x):
    return jax.nn.silu(x)

def _sigmoid(x):
    return jax.nn.sigmoid(x)

def _layernorm(x, axis=-1, eps=1e-05):
    m = jnp.mean(x, axis=axis, keepdims=True)
    v = jnp.var(x, axis=axis, keepdims=True)
    return (x - m) / jnp.sqrt(v + eps)

def _scatter_add(tgt, idx, src, axis=0):
    return tgt.at[idx].add(src)

def _segment_sum(src, seg, n):
    return jax.ops.segment_sum(src, seg, n)
kernel_name = 'mk_gnn_resnorm_d4_gnn_r32_080f7c'

def setup_inputs(seed: int=0):
    np.random.seed(seed)
    _w = jnp.asarray

    def _rec_inputs():
        import jax
        import jax.numpy as jnp
        _gk = jax.random.key(seed)
        x = -0.0009044 + 1 * jax.random.normal(jax.random.fold_in(_gk, 1), (50000, 160), jnp.float32)
        src = jax.random.randint(jax.random.fold_in(_gk, 2), (50000,), 0, 50000, jnp.int32)
        dst = jax.random.randint(jax.random.fold_in(_gk, 3), (50000,), 0, 50000, jnp.int32)
        _o = jnp.argsort(dst, stable=True)
        src = src[_o]
        dst = dst[_o]
        edge_attr_16 = -0.000191324 + 0.999809 * jax.random.normal(jax.random.fold_in(_gk, 12), (50000, 16), jnp.float32)
        edge_attr_3 = 0.00262751 + 0.999568 * jax.random.normal(jax.random.fold_in(_gk, 13), (50000, 3), jnp.float32)
        edge_attr_4 = 0.000126197 + 0.999763 * jax.random.normal(jax.random.fold_in(_gk, 14), (50000, 4), jnp.float32)
        edge_attr_64 = jax.random.uniform(jax.random.fold_in(_gk, 15), (50000, 64), jnp.float32, 0.0, 1)
        edge_attr_8 = 0.000398945 + 1.00003 * jax.random.normal(jax.random.fold_in(_gk, 16), (50000, 8), jnp.float32)
        node_vec1 = jax.random.uniform(jax.random.fold_in(_gk, 17), (50000, 1), jnp.float32, 0.0, 1)
        return (x, src, dst, edge_attr_16, edge_attr_3, edge_attr_4, edge_attr_64, edge_attr_8, node_vec1)
    x, src, dst, edge_attr_16, edge_attr_3, edge_attr_4, edge_attr_64, edge_attr_8, node_vec1 = _rec_inputs()

    def _L0_gnn_setup():
        import jax, jax.numpy as jnp
        import numpy as np
        N, E = (10000, 5000)
        C0, C1 = (64, 32)
        H, A = (8, 8)
        H0, H1 = (8, 4)
        M0, M1 = (128, 64)
        NG, RH = (64, 64)
        WN = C0 + C0 + C1 + C1 + C1
        DS, DV = (C0 + C1, C0 + 2 * C1)
        EPS = 1e-05
        SQ3 = np.float32(np.sqrt(3.0))
        SQ2 = np.float32(np.sqrt(2.0))

        def _split(x):
            return (x[:, :C0], x[:, C0:].reshape(x.shape[0], C1, 3))

        def _merge(s, v):
            return jnp.concatenate([s, v.reshape(v.shape[0], -1)], axis=1)

        def _eq_ln(x, w0, b0, w1):
            s, v = _split(x)
            s = s - s.mean(axis=1, keepdims=True)
            s = s * jax.lax.rsqrt(jnp.square(s).mean(axis=1, keepdims=True) + EPS) * w0 + b0
            v = v * jax.lax.rsqrt(jnp.square(v).mean(axis=(1, 2), keepdims=True) + EPS) * w1[None, :, None]
            return (s, v)

        def _eq_lin(s, v, ws, bs, wv):
            return (s @ ws + bs, jnp.einsum('nud,uk->nkd', v, wv))

        def _ln(x, g, b):
            xc = x - x.mean(-1, keepdims=True)
            return xc * jax.lax.rsqrt(jnp.square(xc).mean(-1, keepdims=True) + EPS) * g + b

        def _smooth_leaky(x, alpha=0.2):
            return 0.5 * (1 + alpha) * x + 0.5 * (1 - alpha) * x * (2.0 * jax.nn.sigmoid(x) - 1.0)

        def _forward(node_input, node_attr, edge_vec, edge_scalars, edge_src, edge_dst, ln1_w0, ln1_b0, ln1_w1, ln2_w0, ln2_b0, ln2_w1, msrc_ws, msrc_wv, mdst_ws, mdst_bs, mdst_wv, rw1, rb1, rg1, rbe1, rw2, rb2, rg2, rbe2, rw3, roff, lin_ws, lin_bs, lin_wv, alpha_dot, proj_ws, proj_bs, proj_wv, f1_ws, f1_bs, f1_wv, f2_ws, f2_bs, f2_wv):
            n = node_input.shape[0]
            s, v = _eq_ln(node_input, ln1_w0, ln1_b0, ln1_w1)
            src_s = s @ msrc_ws
            src_v = jnp.einsum('nud,uk->nkd', v, msrc_wv)
            dst_s = s @ mdst_ws + mdst_bs
            dst_v = jnp.einsum('nud,uk->nkd', v, mdst_wv)
            ms = src_s[edge_src] + dst_s[edge_dst]
            mv = src_v[edge_src] + dst_v[edge_dst]
            h = jax.nn.silu(_ln(edge_scalars @ rw1 + rb1, rg1, rbe1))
            h = jax.nn.silu(_ln(h @ rw2 + rb2, rg2, rbe2))
            w = h @ rw3 + roff
            rhat = edge_vec * jax.lax.rsqrt(jnp.sum(jnp.square(edge_vec), -1, keepdims=True) + 1e-12)
            Y1 = SQ3 * rhat
            w1, w2, w3, w4, w5 = jnp.split(w, [C0, 2 * C0, 2 * C0 + C1, 2 * C0 + 2 * C1], axis=1)
            o0a = w1 * ms
            o0b = w4 * (jnp.einsum('eud,ed->eu', mv, Y1) / SQ3)
            o1a = (w2 * ms)[:, :, None] * Y1[:, None, :]
            o1b = w3[:, :, None] * mv
            o1c = w5[:, :, None] * (jnp.cross(mv, Y1[:, None, :]) / SQ2)
            ds = jnp.concatenate([o0a, o0b], axis=1)
            dv = jnp.concatenate([o1a, o1b, o1c], axis=1)
            ls, lv = _eq_lin(ds, dv, lin_ws, lin_bs, lin_wv)
            e = ls.shape[0]
            alpha = ls[:, :H * A].reshape(e, H, A)
            vs = ls[:, H * A:].reshape(e, H, H0)
            vv = lv.reshape(e, H, H1, 3)
            a = jnp.einsum('ehk,hk->eh', _smooth_leaky(alpha), alpha_dot)
            amax = jax.lax.stop_gradient(jax.ops.segment_max(a, edge_dst, num_segments=n))
            a = jnp.exp(a - amax[edge_dst])
            a = a / (jax.ops.segment_sum(a, edge_dst, num_segments=n)[edge_dst] + 1e-12)
            ns = jax.ops.segment_sum(vs * a[..., None], edge_dst, num_segments=n).reshape(n, H * H0)
            nv = jax.ops.segment_sum(vv * a[..., None, None], edge_dst, num_segments=n).reshape(n, H * H1, 3)
            ps, pv = _eq_lin(ns, nv, proj_ws, proj_bs, proj_wv)
            x = node_input + _merge(ps, pv)
            s2, v2 = _eq_ln(x, ln2_w0, ln2_b0, ln2_w1)
            a0 = node_attr[:, :1]
            fs, fv = _eq_lin(s2, v2, f1_ws, f1_bs, f1_wv)
            fs = fs * a0
            fv = fv * a0[:, :, None]
            sc = jax.nn.silu(fs[:, :M0])
            fv = fv * jax.nn.sigmoid(fs[:, M0:])[:, :, None]
            os_, ov = _eq_lin(sc, fv, f2_ws, f2_bs, f2_wv)
            os_ = os_ * a0
            ov = ov * a0[:, :, None]
            return x + _merge(os_, ov)
        key = jax.random.key(seed)
        ks = iter(jax.random.split(key, 24))

        def nrm(shape, fan):
            return jax.random.normal(next(ks), shape, jnp.float32) / np.float32(np.sqrt(fan))
        inp = {}
        inp['node_input'] = jax.random.normal(next(ks), (N, C0 + 3 * C1), jnp.float32)
        inp['node_attr'] = jnp.ones((N, 1), jnp.float32)
        inp['edge_vec'] = jax.random.normal(next(ks), (E, 3), jnp.float32)
        inp['edge_scalars'] = jax.random.uniform(next(ks), (E, NG), dtype=jnp.float32)
        inp['edge_src'] = jax.random.randint(next(ks), (E,), 0, N)
        inp['edge_dst'] = jax.random.randint(next(ks), (E,), 0, N)
        inp['ln1_w0'] = jnp.ones((C0,), jnp.float32)
        inp['ln1_b0'] = jnp.zeros((C0,), jnp.float32)
        inp['ln1_w1'] = jnp.ones((C1,), jnp.float32)
        inp['ln2_w0'] = jnp.ones((C0,), jnp.float32)
        inp['ln2_b0'] = jnp.zeros((C0,), jnp.float32)
        inp['ln2_w1'] = jnp.ones((C1,), jnp.float32)
        inp['msrc_ws'] = nrm((C0, C0), C0)
        inp['msrc_wv'] = nrm((C1, C1), C1)
        inp['mdst_ws'] = nrm((C0, C0), C0)
        inp['mdst_bs'] = jnp.zeros((C0,), jnp.float32)
        inp['mdst_wv'] = nrm((C1, C1), C1)
        inp['rw1'] = nrm((NG, RH), NG)
        inp['rb1'] = jnp.zeros((RH,), jnp.float32)
        inp['rg1'] = jnp.ones((RH,), jnp.float32)
        inp['rbe1'] = jnp.zeros((RH,), jnp.float32)
        inp['rw2'] = nrm((RH, RH), RH)
        inp['rb2'] = jnp.zeros((RH,), jnp.float32)
        inp['rg2'] = jnp.ones((RH,), jnp.float32)
        inp['rbe2'] = jnp.zeros((RH,), jnp.float32)
        inp['rw3'] = nrm((RH, WN), RH)
        inp['roff'] = 0.1 * jax.random.normal(next(ks), (WN,), jnp.float32)
        inp['lin_ws'] = nrm((DS, H * A + H * H0), DS)
        inp['lin_bs'] = jnp.zeros((H * A + H * H0,), jnp.float32)
        inp['lin_wv'] = nrm((DV, H * H1), DV)
        inp['alpha_dot'] = nrm((H, A), A)
        inp['proj_ws'] = nrm((H * H0, C0), H * H0)
        inp['proj_bs'] = jnp.zeros((C0,), jnp.float32)
        inp['proj_wv'] = nrm((H * H1, C1), H * H1)
        inp['f1_ws'] = nrm((C0, M0 + M1), C0)
        inp['f1_bs'] = jnp.zeros((M0 + M1,), jnp.float32)
        inp['f1_wv'] = nrm((C1, M1), C1)
        inp['f2_ws'] = nrm((M0, C0), M0)
        inp['f2_bs'] = jnp.zeros((C0,), jnp.float32)
        inp['f2_wv'] = nrm((M1, C1), M1)
        return inp
    _L0_gnn_all = _L0_gnn_setup()
    _L0_gnn_in = {k: v for k, v in _L0_gnn_all.items() if k in ('ln1_w0', 'ln1_b0', 'ln1_w1', 'ln2_w0', 'ln2_b0', 'ln2_w1', 'msrc_ws', 'msrc_wv', 'mdst_ws', 'mdst_bs', 'mdst_wv', 'rw1', 'rb1', 'rg1', 'rbe1', 'rw2', 'rb2', 'rg2', 'rbe2', 'rw3', 'roff', 'lin_ws', 'lin_bs', 'lin_wv', 'alpha_dot', 'proj_ws', 'proj_bs', 'proj_wv', 'f1_ws', 'f1_bs', 'f1_wv', 'f2_ws', 'f2_bs', 'f2_wv')}
    del _L0_gnn_all

    def _L1_gnn_setup():
        import jax, jax.numpy as jnp
        import numpy as np
        N = 625
        E = 10000
        MUL0 = 64
        MUL1 = 32
        FC_IN = 16
        FC_H = 64
        WNUM = 192
        key = jax.random.key(seed)
        ks = jax.random.split(key, 16)
        return {'x': jax.random.normal(ks[0], (N, MUL0 + 3 * MUL1), jnp.float32), 'node_attr': jnp.ones((N, 1), jnp.float32), 'edge_scalars': jax.random.normal(ks[1], (E, FC_IN), jnp.float32), 'edge_attr_sh': jax.random.normal(ks[2], (E, 4), jnp.float32), 'edge_src': jax.random.randint(ks[3], (E,), 0, N), 'edge_dst': jax.random.randint(ks[4], (E,), 0, N), 'Wfc1': jax.random.normal(ks[5], (FC_IN, FC_H), jnp.float32), 'Wfc2': jax.random.normal(ks[6], (FC_H, WNUM), jnp.float32), 'Wsc0': jax.random.normal(ks[7], (MUL0, MUL0), jnp.float32), 'Wsc1': jax.random.normal(ks[8], (MUL1, MUL1), jnp.float32), 'Wl1_0': jax.random.normal(ks[9], (MUL0, MUL0), jnp.float32), 'Wl1_1': jax.random.normal(ks[10], (MUL1, MUL1), jnp.float32), 'Wl2_s': jax.random.normal(ks[11], (MUL0 + MUL1, MUL0), jnp.float32), 'Wl2_v': jax.random.normal(ks[12], (MUL0 + MUL1, MUL1), jnp.float32), 'Wa': 0.1 * jax.random.normal(ks[13], (MUL0 + MUL1, 1), jnp.float32)}
    _L1_gnn_all = _L1_gnn_setup()
    _L1_gnn_in = {k: v for k, v in _L1_gnn_all.items() if k in ('Wfc1', 'Wfc2', 'Wsc0', 'Wsc1', 'Wl1_0', 'Wl1_1', 'Wl2_s', 'Wl2_v', 'Wa')}
    del _L1_gnn_all

    def _L2_gnn_setup():
        import jax, jax.numpy as jnp
        import numpy as np
        INV3 = 1.0 / np.sqrt(3.0)

        def _fctp(x_s, x_v, attr, w0, w1):
            s = x_s @ w0 * (1.0 / np.sqrt(x_s.shape[-1])) * attr
            v = jnp.einsum('nud,uw->nwd', x_v, w1) * (1.0 / np.sqrt(x_v.shape[-2])) * attr[..., None]
            return (s, v)
        key = jax.random.key(seed)
        ks = jax.random.split(key, 16)
        N, E = (50000, 25000)
        inp = {'node_input': jax.random.normal(ks[0], (N, 160), jnp.float32), 'node_attr': jnp.ones((N, 1), jnp.float32), 'edge_attr': jax.random.normal(ks[1], (E, 4), jnp.float32), 'edge_scalars': jax.random.normal(ks[2], (E, 8), jnp.float32), 'sc_w0': jax.random.normal(ks[3], (64, 64), jnp.float32), 'sc_w1': jax.random.normal(ks[4], (32, 32), jnp.float32), 'lin1_w0': jax.random.normal(ks[5], (64, 64), jnp.float32), 'lin1_w1': jax.random.normal(ks[6], (32, 32), jnp.float32), 'fc_w1': jax.random.normal(ks[7], (8, 64), jnp.float32), 'fc_w2': jax.random.normal(ks[8], (64, 192), jnp.float32), 'lin2_w0': jax.random.normal(ks[9], (96, 64), jnp.float32), 'lin2_w1': jax.random.normal(ks[10], (96, 32), jnp.float32), 'lin3_w': jax.random.normal(ks[11], (96, 1), jnp.float32), 'edge_src': jax.random.randint(ks[12], (E,), 0, N), 'edge_dst': jax.random.randint(ks[13], (E,), 0, N), 'num_neighbors': 16}
        return inp
    _L2_gnn_all = _L2_gnn_setup()
    _L2_gnn_in = {k: v for k, v in _L2_gnn_all.items() if k in ('sc_w0', 'sc_w1', 'lin1_w0', 'lin1_w1', 'fc_w1', 'fc_w2', 'lin2_w0', 'lin2_w1', 'lin3_w')}
    del _L2_gnn_all

    def _L3_gnn_setup():
        import jax, jax.numpy as jnp
        import numpy as np
        N, E = (1250, 20000)
        S_IN, V_IN = (64, 32)
        S_MID, V_MID = (96, 128)
        S_OUT, V_OUT = (96, 32)
        R = 64
        FC_HID = 64
        W_NUMEL = 64 + 64 + 32 + 32 + 32
        NUM_NEIGHBORS = 16.0

        def _inv(d):
            return 1.0 / jnp.sqrt(jnp.float32(d))

        def _forward(node_features, node_attr, edge_attr, edge_scalars, lin1_ws, lin1_wv, fc_w1, fc_w2, sc_ws, sc_wv, lin2_ws, lin2_wv, edge_src, edge_dst):
            n = node_features.shape[0]
            s = node_features[:, :S_IN]
            v = node_features[:, S_IN:].reshape(n, V_IN, 3)
            a = node_attr
            sc_s = s @ sc_ws * a * _inv(S_IN)
            sc_v = jnp.einsum('nci,cd->ndi', v, sc_wv) * a[:, :, None] * _inv(V_IN)
            h_s = s @ lin1_ws * a * _inv(S_IN)
            h_v = jnp.einsum('nci,cd->ndi', v, lin1_wv) * a[:, :, None] * _inv(V_IN)
            hid = jax.nn.silu(edge_scalars @ fc_w1 * _inv(R))
            w = hid @ fc_w2 * _inv(FC_HID)
            w1, w2, w3, w4, w5 = jnp.split(w, [64, 128, 160, 192], axis=-1)
            es = h_s[edge_src]
            ev = h_v[edge_src]
            e0 = edge_attr[:, :1]
            e1 = edge_attr[:, 1:4]
            m_s1 = w1 * es * e0
            m_s2 = w4 * jnp.einsum('eci,ei->ec', ev, e1) * _inv(3)
            m_v1 = (w2 * es)[:, :, None] * e1[:, None, :]
            m_v2 = w3[:, :, None] * ev * e0[:, :, None]
            m_v3 = w5[:, :, None] * jnp.cross(ev, e1[:, None, :]) * _inv(2)
            mid_s = jnp.concatenate([m_s1, m_s2], axis=-1)
            mid_v = jnp.concatenate([m_v1, m_v2, m_v3], axis=1)
            inv_nn = 1.0 / jnp.sqrt(jnp.float32(NUM_NEIGHBORS))
            agg_s = jax.ops.segment_sum(mid_s, edge_dst, num_segments=n) * inv_nn
            agg_v = jax.ops.segment_sum(mid_v, edge_dst, num_segments=n) * inv_nn
            o_s = agg_s @ lin2_ws * a * _inv(S_MID)
            o_v = jnp.einsum('nci,cd->ndi', agg_v, lin2_wv) * a[:, :, None] * _inv(V_MID)
            pre_s = sc_s + o_s
            pre_v = sc_v + o_v
            scalars = jax.nn.silu(pre_s[:, :64])
            gates = jax.nn.sigmoid(pre_s[:, 64:96])
            gated = gates[:, :, None] * pre_v
            return jnp.concatenate([scalars, gated.reshape(n, 3 * V_OUT)], axis=-1)
        key = jax.random.key(seed)
        ks = jax.random.split(key, 13)
        return {'node_features': jax.random.normal(ks[0], (N, S_IN + 3 * V_IN), jnp.float32), 'node_attr': jnp.ones((N, 1), jnp.float32), 'edge_src': jax.random.randint(ks[1], (E,), 0, N), 'edge_dst': jax.random.randint(ks[2], (E,), 0, N), 'edge_attr': jax.random.normal(ks[3], (E, 4), jnp.float32), 'edge_scalars': jax.random.normal(ks[4], (E, R), jnp.float32), 'lin1_ws': jax.random.normal(ks[5], (S_IN, S_IN), jnp.float32), 'lin1_wv': jax.random.normal(ks[6], (V_IN, V_IN), jnp.float32), 'fc_w1': jax.random.normal(ks[7], (R, FC_HID), jnp.float32), 'fc_w2': jax.random.normal(ks[8], (FC_HID, W_NUMEL), jnp.float32), 'sc_ws': jax.random.normal(ks[9], (S_IN, S_OUT), jnp.float32), 'sc_wv': jax.random.normal(ks[10], (V_IN, V_OUT), jnp.float32), 'lin2_ws': jax.random.normal(ks[11], (S_MID, S_OUT), jnp.float32), 'lin2_wv': jax.random.normal(ks[12], (V_MID, V_OUT), jnp.float32)}
    _L3_gnn_all = _L3_gnn_setup()
    _L3_gnn_in = {k: v for k, v in _L3_gnn_all.items() if k in ('lin1_ws', 'lin1_wv', 'fc_w1', 'fc_w2', 'sc_ws', 'sc_wv', 'lin2_ws', 'lin2_wv')}
    del _L3_gnn_all
    return {'x': x, 'src': src, 'dst': dst, 'edge_attr_16': edge_attr_16, 'edge_attr_3': edge_attr_3, 'edge_attr_4': edge_attr_4, 'edge_attr_64': edge_attr_64, 'edge_attr_8': edge_attr_8, 'node_vec1': node_vec1, 'L0_gnn_ln1_w0': _L0_gnn_in['ln1_w0'], 'L0_gnn_ln1_b0': _L0_gnn_in['ln1_b0'], 'L0_gnn_ln1_w1': _L0_gnn_in['ln1_w1'], 'L0_gnn_ln2_w0': _L0_gnn_in['ln2_w0'], 'L0_gnn_ln2_b0': _L0_gnn_in['ln2_b0'], 'L0_gnn_ln2_w1': _L0_gnn_in['ln2_w1'], 'L0_gnn_msrc_ws': _L0_gnn_in['msrc_ws'], 'L0_gnn_msrc_wv': _L0_gnn_in['msrc_wv'], 'L0_gnn_mdst_ws': _L0_gnn_in['mdst_ws'], 'L0_gnn_mdst_bs': _L0_gnn_in['mdst_bs'], 'L0_gnn_mdst_wv': _L0_gnn_in['mdst_wv'], 'L0_gnn_rw1': _L0_gnn_in['rw1'], 'L0_gnn_rb1': _L0_gnn_in['rb1'], 'L0_gnn_rg1': _L0_gnn_in['rg1'], 'L0_gnn_rbe1': _L0_gnn_in['rbe1'], 'L0_gnn_rw2': _L0_gnn_in['rw2'], 'L0_gnn_rb2': _L0_gnn_in['rb2'], 'L0_gnn_rg2': _L0_gnn_in['rg2'], 'L0_gnn_rbe2': _L0_gnn_in['rbe2'], 'L0_gnn_rw3': _L0_gnn_in['rw3'], 'L0_gnn_roff': _L0_gnn_in['roff'], 'L0_gnn_lin_ws': _L0_gnn_in['lin_ws'], 'L0_gnn_lin_bs': _L0_gnn_in['lin_bs'], 'L0_gnn_lin_wv': _L0_gnn_in['lin_wv'], 'L0_gnn_alpha_dot': _L0_gnn_in['alpha_dot'], 'L0_gnn_proj_ws': _L0_gnn_in['proj_ws'], 'L0_gnn_proj_bs': _L0_gnn_in['proj_bs'], 'L0_gnn_proj_wv': _L0_gnn_in['proj_wv'], 'L0_gnn_f1_ws': _L0_gnn_in['f1_ws'], 'L0_gnn_f1_bs': _L0_gnn_in['f1_bs'], 'L0_gnn_f1_wv': _L0_gnn_in['f1_wv'], 'L0_gnn_f2_ws': _L0_gnn_in['f2_ws'], 'L0_gnn_f2_bs': _L0_gnn_in['f2_bs'], 'L0_gnn_f2_wv': _L0_gnn_in['f2_wv'], 'L1_gnn_Wfc1': _L1_gnn_in['Wfc1'], 'L1_gnn_Wfc2': _L1_gnn_in['Wfc2'], 'L1_gnn_Wsc0': _L1_gnn_in['Wsc0'], 'L1_gnn_Wsc1': _L1_gnn_in['Wsc1'], 'L1_gnn_Wl1_0': _L1_gnn_in['Wl1_0'], 'L1_gnn_Wl1_1': _L1_gnn_in['Wl1_1'], 'L1_gnn_Wl2_s': _L1_gnn_in['Wl2_s'], 'L1_gnn_Wl2_v': _L1_gnn_in['Wl2_v'], 'L1_gnn_Wa': _L1_gnn_in['Wa'], 'L2_gnn_sc_w0': _L2_gnn_in['sc_w0'], 'L2_gnn_sc_w1': _L2_gnn_in['sc_w1'], 'L2_gnn_lin1_w0': _L2_gnn_in['lin1_w0'], 'L2_gnn_lin1_w1': _L2_gnn_in['lin1_w1'], 'L2_gnn_fc_w1': _L2_gnn_in['fc_w1'], 'L2_gnn_fc_w2': _L2_gnn_in['fc_w2'], 'L2_gnn_lin2_w0': _L2_gnn_in['lin2_w0'], 'L2_gnn_lin2_w1': _L2_gnn_in['lin2_w1'], 'L2_gnn_lin3_w': _L2_gnn_in['lin3_w'], 'L3_gnn_lin1_ws': _L3_gnn_in['lin1_ws'], 'L3_gnn_lin1_wv': _L3_gnn_in['lin1_wv'], 'L3_gnn_fc_w1': _L3_gnn_in['fc_w1'], 'L3_gnn_fc_w2': _L3_gnn_in['fc_w2'], 'L3_gnn_sc_ws': _L3_gnn_in['sc_ws'], 'L3_gnn_sc_wv': _L3_gnn_in['sc_wv'], 'L3_gnn_lin2_ws': _L3_gnn_in['lin2_ws'], 'L3_gnn_lin2_wv': _L3_gnn_in['lin2_wv']}

def reference(x, src, dst, edge_attr_16, edge_attr_3, edge_attr_4, edge_attr_64, edge_attr_8, node_vec1, L0_gnn_ln1_w0, L0_gnn_ln1_b0, L0_gnn_ln1_w1, L0_gnn_ln2_w0, L0_gnn_ln2_b0, L0_gnn_ln2_w1, L0_gnn_msrc_ws, L0_gnn_msrc_wv, L0_gnn_mdst_ws, L0_gnn_mdst_bs, L0_gnn_mdst_wv, L0_gnn_rw1, L0_gnn_rb1, L0_gnn_rg1, L0_gnn_rbe1, L0_gnn_rw2, L0_gnn_rb2, L0_gnn_rg2, L0_gnn_rbe2, L0_gnn_rw3, L0_gnn_roff, L0_gnn_lin_ws, L0_gnn_lin_bs, L0_gnn_lin_wv, L0_gnn_alpha_dot, L0_gnn_proj_ws, L0_gnn_proj_bs, L0_gnn_proj_wv, L0_gnn_f1_ws, L0_gnn_f1_bs, L0_gnn_f1_wv, L0_gnn_f2_ws, L0_gnn_f2_bs, L0_gnn_f2_wv, L1_gnn_Wfc1, L1_gnn_Wfc2, L1_gnn_Wsc0, L1_gnn_Wsc1, L1_gnn_Wl1_0, L1_gnn_Wl1_1, L1_gnn_Wl2_s, L1_gnn_Wl2_v, L1_gnn_Wa, L2_gnn_sc_w0, L2_gnn_sc_w1, L2_gnn_lin1_w0, L2_gnn_lin1_w1, L2_gnn_fc_w1, L2_gnn_fc_w2, L2_gnn_lin2_w0, L2_gnn_lin2_w1, L2_gnn_lin3_w, L3_gnn_lin1_ws, L3_gnn_lin1_wv, L3_gnn_fc_w1, L3_gnn_fc_w2, L3_gnn_sc_ws, L3_gnn_sc_wv, L3_gnn_lin2_ws, L3_gnn_lin2_wv):
    import jax
    import jax.numpy as jnp

    def _L0_gnn_ref(node_input, node_attr, edge_vec, edge_scalars, edge_src, edge_dst, ln1_w0, ln1_b0, ln1_w1, ln2_w0, ln2_b0, ln2_w1, msrc_ws, msrc_wv, mdst_ws, mdst_bs, mdst_wv, rw1, rb1, rg1, rbe1, rw2, rb2, rg2, rbe2, rw3, roff, lin_ws, lin_bs, lin_wv, alpha_dot, proj_ws, proj_bs, proj_wv, f1_ws, f1_bs, f1_wv, f2_ws, f2_bs, f2_wv):
        import jax, jax.numpy as jnp
        import numpy as np
        N, E = (10000, 5000)
        C0, C1 = (64, 32)
        H, A = (8, 8)
        H0, H1 = (8, 4)
        M0, M1 = (128, 64)
        NG, RH = (64, 64)
        WN = C0 + C0 + C1 + C1 + C1
        DS, DV = (C0 + C1, C0 + 2 * C1)
        EPS = 1e-05
        SQ3 = np.float32(np.sqrt(3.0))
        SQ2 = np.float32(np.sqrt(2.0))

        def _split(x):
            return (x[:, :C0], x[:, C0:].reshape(x.shape[0], C1, 3))

        def _merge(s, v):
            return jnp.concatenate([s, v.reshape(v.shape[0], -1)], axis=1)

        def _eq_ln(x, w0, b0, w1):
            s, v = _split(x)
            s = s - s.mean(axis=1, keepdims=True)
            s = s * jax.lax.rsqrt(jnp.square(s).mean(axis=1, keepdims=True) + EPS) * w0 + b0
            v = v * jax.lax.rsqrt(jnp.square(v).mean(axis=(1, 2), keepdims=True) + EPS) * w1[None, :, None]
            return (s, v)

        def _eq_lin(s, v, ws, bs, wv):
            return (s @ ws + bs, jnp.einsum('nud,uk->nkd', v, wv))

        def _ln(x, g, b):
            xc = x - x.mean(-1, keepdims=True)
            return xc * jax.lax.rsqrt(jnp.square(xc).mean(-1, keepdims=True) + EPS) * g + b

        def _smooth_leaky(x, alpha=0.2):
            return 0.5 * (1 + alpha) * x + 0.5 * (1 - alpha) * x * (2.0 * jax.nn.sigmoid(x) - 1.0)

        def _forward(node_input, node_attr, edge_vec, edge_scalars, edge_src, edge_dst, ln1_w0, ln1_b0, ln1_w1, ln2_w0, ln2_b0, ln2_w1, msrc_ws, msrc_wv, mdst_ws, mdst_bs, mdst_wv, rw1, rb1, rg1, rbe1, rw2, rb2, rg2, rbe2, rw3, roff, lin_ws, lin_bs, lin_wv, alpha_dot, proj_ws, proj_bs, proj_wv, f1_ws, f1_bs, f1_wv, f2_ws, f2_bs, f2_wv):
            n = node_input.shape[0]
            s, v = _eq_ln(node_input, ln1_w0, ln1_b0, ln1_w1)
            src_s = s @ msrc_ws
            src_v = jnp.einsum('nud,uk->nkd', v, msrc_wv)
            dst_s = s @ mdst_ws + mdst_bs
            dst_v = jnp.einsum('nud,uk->nkd', v, mdst_wv)
            ms = src_s[edge_src] + dst_s[edge_dst]
            mv = src_v[edge_src] + dst_v[edge_dst]
            h = jax.nn.silu(_ln(edge_scalars @ rw1 + rb1, rg1, rbe1))
            h = jax.nn.silu(_ln(h @ rw2 + rb2, rg2, rbe2))
            w = h @ rw3 + roff
            rhat = edge_vec * jax.lax.rsqrt(jnp.sum(jnp.square(edge_vec), -1, keepdims=True) + 1e-12)
            Y1 = SQ3 * rhat
            w1, w2, w3, w4, w5 = jnp.split(w, [C0, 2 * C0, 2 * C0 + C1, 2 * C0 + 2 * C1], axis=1)
            o0a = w1 * ms
            o0b = w4 * (jnp.einsum('eud,ed->eu', mv, Y1) / SQ3)
            o1a = (w2 * ms)[:, :, None] * Y1[:, None, :]
            o1b = w3[:, :, None] * mv
            o1c = w5[:, :, None] * (jnp.cross(mv, Y1[:, None, :]) / SQ2)
            ds = jnp.concatenate([o0a, o0b], axis=1)
            dv = jnp.concatenate([o1a, o1b, o1c], axis=1)
            ls, lv = _eq_lin(ds, dv, lin_ws, lin_bs, lin_wv)
            e = ls.shape[0]
            alpha = ls[:, :H * A].reshape(e, H, A)
            vs = ls[:, H * A:].reshape(e, H, H0)
            vv = lv.reshape(e, H, H1, 3)
            a = jnp.einsum('ehk,hk->eh', _smooth_leaky(alpha), alpha_dot)
            amax = jax.lax.stop_gradient(jax.ops.segment_max(a, edge_dst, num_segments=n))
            a = jnp.exp(a - amax[edge_dst])
            a = a / (jax.ops.segment_sum(a, edge_dst, num_segments=n)[edge_dst] + 1e-12)
            ns = jax.ops.segment_sum(vs * a[..., None], edge_dst, num_segments=n).reshape(n, H * H0)
            nv = jax.ops.segment_sum(vv * a[..., None, None], edge_dst, num_segments=n).reshape(n, H * H1, 3)
            ps, pv = _eq_lin(ns, nv, proj_ws, proj_bs, proj_wv)
            x = node_input + _merge(ps, pv)
            s2, v2 = _eq_ln(x, ln2_w0, ln2_b0, ln2_w1)
            a0 = node_attr[:, :1]
            fs, fv = _eq_lin(s2, v2, f1_ws, f1_bs, f1_wv)
            fs = fs * a0
            fv = fv * a0[:, :, None]
            sc = jax.nn.silu(fs[:, :M0])
            fv = fv * jax.nn.sigmoid(fs[:, M0:])[:, :, None]
            os_, ov = _eq_lin(sc, fv, f2_ws, f2_bs, f2_wv)
            os_ = os_ * a0
            ov = ov * a0[:, :, None]
            return x + _merge(os_, ov)
        return _forward(node_input, node_attr, edge_vec, edge_scalars, edge_src, edge_dst, ln1_w0, ln1_b0, ln1_w1, ln2_w0, ln2_b0, ln2_w1, msrc_ws, msrc_wv, mdst_ws, mdst_bs, mdst_wv, rw1, rb1, rg1, rbe1, rw2, rb2, rg2, rbe2, rw3, roff, lin_ws, lin_bs, lin_wv, alpha_dot, proj_ws, proj_bs, proj_wv, f1_ws, f1_bs, f1_wv, f2_ws, f2_bs, f2_wv)

    def _L1_gnn_ref(x, node_attr, edge_scalars, edge_attr_sh, edge_src, edge_dst, Wfc1, Wfc2, Wsc0, Wsc1, Wl1_0, Wl1_1, Wl2_s, Wl2_v, Wa):
        import jax, jax.numpy as jnp
        import numpy as np
        N = 625
        E = 10000
        MUL0 = 64
        MUL1 = 32
        FC_IN = 16
        FC_H = 64
        WNUM = 192
        n = x.shape[0]
        x0 = x[:, :MUL0]
        x1 = x[:, MUL0:].reshape(n, MUL1, 3)
        a = node_attr
        h = jax.nn.silu(edge_scalars @ (Wfc1 / jnp.sqrt(jnp.float32(FC_IN))))
        w = h @ (Wfc2 / jnp.sqrt(jnp.float32(FC_H)))
        w0 = w[:, :64]
        w1 = w[:, 64:128]
        w2 = w[:, 128:160]
        w3 = w[:, 160:192]
        inv8 = 1.0 / jnp.sqrt(jnp.float32(MUL0))
        inv32 = 1.0 / jnp.sqrt(jnp.float32(MUL1))
        sc = jnp.concatenate([x0 @ Wsc0 * a * inv8, (jnp.einsum('num,uv->nvm', x1, Wsc1) * a[..., None] * inv32).reshape(n, 3 * MUL1)], axis=1)
        f0 = x0 @ Wl1_0 * a * inv8
        f1 = jnp.einsum('num,uv->nvm', x1, Wl1_1) * a[..., None] * inv32
        e0 = f0[edge_src]
        e1 = f1[edge_src]
        sh0 = edge_attr_sh[:, :1]
        sh1 = edge_attr_sh[:, 1:4]
        mid0 = w0 * e0 * sh0
        mid1 = w3 * jnp.einsum('eum,em->eu', e1, sh1) / jnp.sqrt(3.0)
        mid2 = w1[:, :, None] * e0[:, :, None] * sh1[:, None, :]
        mid3 = w2[:, :, None] * e1 * sh0[:, :, None]
        cnt = jnp.clip(jax.ops.segment_sum(jnp.ones(edge_dst.shape, x.dtype), edge_dst, num_segments=n), 1.0)

        def smean(v):
            s = jax.ops.segment_sum(v, edge_dst, num_segments=n)
            return s / cnt.reshape((n,) + (1,) * (v.ndim - 1))
        n0, n1 = (smean(mid0), smean(mid1))
        n2, n3 = (smean(mid2), smean(mid3))
        scal = jnp.concatenate([n0, n1], axis=1)
        vec = jnp.concatenate([n2, n3], axis=1)
        inv96 = 1.0 / jnp.sqrt(jnp.float32(MUL0 + MUL1))
        alpha = scal @ Wa * a * inv96
        out_s = scal @ Wl2_s * a * inv96
        out_v = jnp.einsum('num,uv->nvm', vec, Wl2_v) * a[..., None] * inv96
        conv = jnp.concatenate([out_s, out_v.reshape(n, 3 * MUL1)], axis=1)
        return sc + alpha * conv

    def _L2_gnn_ref(node_input, node_attr, edge_attr, edge_scalars, sc_w0, sc_w1, lin1_w0, lin1_w1, fc_w1, fc_w2, lin2_w0, lin2_w1, lin3_w, edge_src, edge_dst, num_neighbors):
        import jax, jax.numpy as jnp
        import numpy as np
        INV3 = 1.0 / np.sqrt(3.0)

        def _fctp(x_s, x_v, attr, w0, w1):
            s = x_s @ w0 * (1.0 / np.sqrt(x_s.shape[-1])) * attr
            v = jnp.einsum('nud,uw->nwd', x_v, w1) * (1.0 / np.sqrt(x_v.shape[-2])) * attr[..., None]
            return (s, v)
        N = node_input.shape[0]
        h = jax.nn.silu(edge_scalars @ fc_w1 * (1.0 / np.sqrt(8.0)))
        weight = h @ fc_w2 * (1.0 / np.sqrt(64.0))
        xs, xv = (node_input[:, :64], node_input[:, 64:].reshape(N, 32, 3))
        sc_s, sc_v = _fctp(xs, xv, node_attr, sc_w0, sc_w1)
        f_s, f_v = _fctp(xs, xv, node_attr, lin1_w0, lin1_w1)
        gs = f_s[edge_src]
        gv = f_v[edge_src]
        ys, yv = (edge_attr[:, :1], edge_attr[:, 1:])
        w1_, w2_ = (weight[:, :64], weight[:, 64:128])
        w3_, w4_ = (weight[:, 128:160], weight[:, 160:192])
        m0a = gs * ys * w1_
        m0b = jnp.sum(gv * yv[:, None, :], -1) * INV3 * w4_
        m1a = gs[..., None] * yv[:, None, :] * w2_[..., None]
        m1b = gv * ys[..., None] * w3_[..., None]
        E = m0a.shape[0]
        edge_feat = jnp.concatenate([m0a, m0b, m1a.reshape(E, 192), m1b.reshape(E, 96)], -1)
        mid = jax.ops.segment_sum(edge_feat, edge_dst, num_segments=N)
        mid = mid / np.sqrt(float(num_neighbors))
        mid_s, mid_v = (mid[:, :96], mid[:, 96:].reshape(N, 96, 3))
        c_s, c_v = _fctp(mid_s, mid_v, node_attr, lin2_w0, lin2_w1)
        conv = jnp.concatenate([c_s, c_v.reshape(N, -1)], -1)
        scfeat = jnp.concatenate([sc_s, sc_v.reshape(N, -1)], -1)
        angle = 0.1 * (mid_s @ lin3_w) * (1.0 / np.sqrt(96.0)) * node_attr
        return jnp.cos(angle) * scfeat + jnp.sin(angle) * conv

    def _L3_gnn_ref(node_features, node_attr, edge_src, edge_dst, edge_attr, edge_scalars, lin1_ws, lin1_wv, fc_w1, fc_w2, sc_ws, sc_wv, lin2_ws, lin2_wv):
        import jax, jax.numpy as jnp
        import numpy as np
        N, E = (1250, 20000)
        S_IN, V_IN = (64, 32)
        S_MID, V_MID = (96, 128)
        S_OUT, V_OUT = (96, 32)
        R = 64
        FC_HID = 64
        W_NUMEL = 64 + 64 + 32 + 32 + 32
        NUM_NEIGHBORS = 16.0

        def _inv(d):
            return 1.0 / jnp.sqrt(jnp.float32(d))

        def _forward(node_features, node_attr, edge_attr, edge_scalars, lin1_ws, lin1_wv, fc_w1, fc_w2, sc_ws, sc_wv, lin2_ws, lin2_wv, edge_src, edge_dst):
            n = node_features.shape[0]
            s = node_features[:, :S_IN]
            v = node_features[:, S_IN:].reshape(n, V_IN, 3)
            a = node_attr
            sc_s = s @ sc_ws * a * _inv(S_IN)
            sc_v = jnp.einsum('nci,cd->ndi', v, sc_wv) * a[:, :, None] * _inv(V_IN)
            h_s = s @ lin1_ws * a * _inv(S_IN)
            h_v = jnp.einsum('nci,cd->ndi', v, lin1_wv) * a[:, :, None] * _inv(V_IN)
            hid = jax.nn.silu(edge_scalars @ fc_w1 * _inv(R))
            w = hid @ fc_w2 * _inv(FC_HID)
            w1, w2, w3, w4, w5 = jnp.split(w, [64, 128, 160, 192], axis=-1)
            es = h_s[edge_src]
            ev = h_v[edge_src]
            e0 = edge_attr[:, :1]
            e1 = edge_attr[:, 1:4]
            m_s1 = w1 * es * e0
            m_s2 = w4 * jnp.einsum('eci,ei->ec', ev, e1) * _inv(3)
            m_v1 = (w2 * es)[:, :, None] * e1[:, None, :]
            m_v2 = w3[:, :, None] * ev * e0[:, :, None]
            m_v3 = w5[:, :, None] * jnp.cross(ev, e1[:, None, :]) * _inv(2)
            mid_s = jnp.concatenate([m_s1, m_s2], axis=-1)
            mid_v = jnp.concatenate([m_v1, m_v2, m_v3], axis=1)
            inv_nn = 1.0 / jnp.sqrt(jnp.float32(NUM_NEIGHBORS))
            agg_s = jax.ops.segment_sum(mid_s, edge_dst, num_segments=n) * inv_nn
            agg_v = jax.ops.segment_sum(mid_v, edge_dst, num_segments=n) * inv_nn
            o_s = agg_s @ lin2_ws * a * _inv(S_MID)
            o_v = jnp.einsum('nci,cd->ndi', agg_v, lin2_wv) * a[:, :, None] * _inv(V_MID)
            pre_s = sc_s + o_s
            pre_v = sc_v + o_v
            scalars = jax.nn.silu(pre_s[:, :64])
            gates = jax.nn.sigmoid(pre_s[:, 64:96])
            gated = gates[:, :, None] * pre_v
            return jnp.concatenate([scalars, gated.reshape(n, 3 * V_OUT)], axis=-1)
        return _forward(node_features, node_attr, edge_attr, edge_scalars, lin1_ws, lin1_wv, fc_w1, fc_w2, sc_ws, sc_wv, lin2_ws, lin2_wv, edge_src, edge_dst)
    x = _layernorm(x + _L0_gnn_ref(x, node_vec1, edge_attr_3, edge_attr_64, src, dst, L0_gnn_ln1_w0, L0_gnn_ln1_b0, L0_gnn_ln1_w1, L0_gnn_ln2_w0, L0_gnn_ln2_b0, L0_gnn_ln2_w1, L0_gnn_msrc_ws, L0_gnn_msrc_wv, L0_gnn_mdst_ws, L0_gnn_mdst_bs, L0_gnn_mdst_wv, L0_gnn_rw1, L0_gnn_rb1, L0_gnn_rg1, L0_gnn_rbe1, L0_gnn_rw2, L0_gnn_rb2, L0_gnn_rg2, L0_gnn_rbe2, L0_gnn_rw3, L0_gnn_roff, L0_gnn_lin_ws, L0_gnn_lin_bs, L0_gnn_lin_wv, L0_gnn_alpha_dot, L0_gnn_proj_ws, L0_gnn_proj_bs, L0_gnn_proj_wv, L0_gnn_f1_ws, L0_gnn_f1_bs, L0_gnn_f1_wv, L0_gnn_f2_ws, L0_gnn_f2_bs, L0_gnn_f2_wv), axis=-1)
    x = _layernorm(x + _L1_gnn_ref(x, node_vec1, edge_attr_16, edge_attr_4, src, dst, L1_gnn_Wfc1, L1_gnn_Wfc2, L1_gnn_Wsc0, L1_gnn_Wsc1, L1_gnn_Wl1_0, L1_gnn_Wl1_1, L1_gnn_Wl2_s, L1_gnn_Wl2_v, L1_gnn_Wa), axis=-1)
    x = _layernorm(x + _L2_gnn_ref(x, node_vec1, edge_attr_4, edge_attr_8, L2_gnn_sc_w0, L2_gnn_sc_w1, L2_gnn_lin1_w0, L2_gnn_lin1_w1, L2_gnn_fc_w1, L2_gnn_fc_w2, L2_gnn_lin2_w0, L2_gnn_lin2_w1, L2_gnn_lin3_w, src, dst, 16), axis=-1)
    x = _layernorm(x + _L3_gnn_ref(x, node_vec1, src, dst, edge_attr_4, edge_attr_64, L3_gnn_lin1_ws, L3_gnn_lin1_wv, L3_gnn_fc_w1, L3_gnn_fc_w2, L3_gnn_sc_ws, L3_gnn_sc_wv, L3_gnn_lin2_ws, L3_gnn_lin2_wv), axis=-1)
    return x

_drawn_inputs = setup_inputs


def setup_inputs(seed=0):
    import zlib

    import numpy as np

    out = dict(_drawn_inputs(seed))
    spreads = {'L0_gnn_ln1_w0': (1.0, 0.2),
     'L0_gnn_ln1_b0': (0.0, 0.392),
     'L0_gnn_ln1_w1': (1.0, 0.2),
     'L0_gnn_ln2_w0': (1.0, 0.6),
     'L0_gnn_ln2_b0': (0.0, 0.8),
     'L0_gnn_ln2_w1': (1.0, 0.6),
     'L0_gnn_mdst_bs': (0.0, 0.576),
     'L0_gnn_rb1': (0.0, 0.1),
     'L0_gnn_rg1': (1.0, 0.2),
     'L0_gnn_rbe1': (0.0, 0.1),
     'L0_gnn_rb2': (0.0, 0.1),
     'L0_gnn_rg2': (1.0, 0.2),
     'L0_gnn_rbe2': (0.0, 0.1),
     'L0_gnn_lin_bs': (0.0, 0.396),
     'L0_gnn_proj_bs': (0.0, 0.272),
     'L0_gnn_f1_bs': (0.0, 0.8),
     'L0_gnn_f2_bs': (0.0, 0.505)}
    factors = {'edge_attr_16': 8.0,
     'edge_attr_4': 3.54,
     'edge_attr_8': 8.0,
     'L1_gnn_Wfc1': 8.0,
     'L1_gnn_Wfc2': 8.0,
     'L1_gnn_Wl1_0': 8.0,
     'L1_gnn_Wl1_1': 8.0,
     'L1_gnn_Wl2_s': 8.0,
     'L1_gnn_Wl2_v': 8.0,
     'L1_gnn_Wa': 8.0,
     'L2_gnn_lin1_w0': 8.0,
     'L2_gnn_lin1_w1': 8.0,
     'L2_gnn_fc_w1': 8.0,
     'L2_gnn_fc_w2': 8.0,
     'L2_gnn_lin2_w0': 8.0,
     'L2_gnn_lin2_w1': 8.0,
     'L2_gnn_lin3_w': 8.0,
     'L3_gnn_lin1_ws': 5.017,
     'L3_gnn_lin1_wv': 5.148,
     'L3_gnn_fc_w1': 4.346,
     'L3_gnn_fc_w2': 4.096,
     'L3_gnn_lin2_ws': 5.206,
     'L3_gnn_lin2_wv': 5.294}
    for name, (base, spread) in spreads.items():
        noise = np.random.default_rng([zlib.crc32(name.encode()), seed]).standard_normal(out[name].shape)
        drawn = base * np.exp(spread * noise) if base else spread * noise
        out[name] = jnp.asarray(drawn.astype(out[name].dtype))
    for name, factor in factors.items():
        out[name] = (out[name] * factor).astype(out[name].dtype)
    return out
```

```python
from contextlib import ExitStack

import numpy as np
import concourse.bass as bass
from concourse import mybir

F32 = mybir.dt.float32
I32 = mybir.dt.int32
ALU = mybir.AluOpType
ACT = mybir.ActivationFunctionType
AX_X = mybir.AxisListType.X

P = 128
CHUNK = 512
TILES = CHUNK // P
C0, C1 = 64, 32
D = C0 + 3 * C1
ROW = D + 1
AGG = 192
HEADS = 8
SKIP = float(1 << 23)
FIX_BLOCKS = 4
NEG = 1.0e30

SHAPES = {
    "ident": (128, 128),
    "ones": (128, 512),
    "ln1_s": (65, 66), "ln1_v": (96, 1),
    "sd_s": (65, 128), "sd_v": (96, 192),
    "rw1": (65, 64), "rg1": (128, 64), "rbe1": (128, 64),
    "rw2": (65, 64), "rg2": (128, 64), "rbe2": (128, 64),
    "rw3": (65, 224),
    "lin_s": (97, 128), "lin_v": (128, 32), "adot": (64, 8),
    "proj_s": (65, 64), "proj_v": (96, 96),
    "ln2_s": (65, 66), "ln2_v": (96, 1),
    "f1_s": (65, 128), "f1_g": (65, 128), "f1_v": (96, 192),
    "f2_s": (128, 64), "f2_b": (1, 64), "f2_v": (128, 64),
    "e_s1": (64, 64), "e_v1": (96, 96), "fc1_1": (16, 64), "fc2_1": (64, 192),
    "post_s1": (97, 66), "post_v1": (96, 32), "sc_s1": (64, 64), "sc_v1": (96, 96),
    "e_s2": (64, 64), "e_v2": (96, 96), "fc1_2": (8, 64), "fc2_2": (64, 192),
    "post_s2": (96, 65), "post_v2": (96, 32), "sc_s2": (64, 64), "sc_v2": (96, 96),
    "e_s3": (64, 64), "e_v3": (96, 96), "fc1_3": (64, 64), "fc2_3": (64, 224),
    "post_s3": (96, 96), "post_v3": (128, 32), "sc_s3": (64, 96), "sc_v3": (96, 96),
}
OFFSETS = {}
WCOLS = 0
for _name, (_r, _c) in SHAPES.items():
    OFFSETS[_name] = WCOLS
    WCOLS += _c

I8 = 1.0 / 8.0
I32C = 1.0 / float(np.sqrt(32.0))
I96 = 1.0 / float(np.sqrt(96.0))
I3 = 1.0 / float(np.sqrt(3.0))
S3 = float(np.sqrt(3.0))
SCALES = [
    ("rw2", (0, 64), 0.5), ("rw3", (0, 64), 0.5),
    ("lin_v", (0, 64), S3), ("lin_v", (96, 128), S3 / float(np.sqrt(2.0))),
    ("f2_s", (0, 128), 0.5), ("f2_v", (0, 128), 0.5),
    ("e_s1", (0, 64), I8), ("e_v1", (0, 96), I32C), ("fc2_1", (0, 64), I8),
    ("post_v1", (0, 96), I96), ("sc_s1", (0, 64), I8), ("sc_v1", (0, 96), I32C),
    ("post_s1", (0, 64), I96), ("post_s1", (64, 96), I96 * I3),
    ("e_s2", (0, 64), I8), ("e_v2", (0, 96), I32C), ("fc2_2", (0, 64), I8),
    ("post_v2", (0, 96), I96 / 4), ("sc_s2", (0, 64), I8), ("sc_v2", (0, 96), I32C),
    ("post_s2", (0, 64), I96 / 4), ("post_s2", (64, 96), I96 * I3 / 4),
    ("e_s3", (0, 64), I8), ("e_v3", (0, 96), I32C), ("fc2_3", (0, 64), I8),
    ("post_s3", (0, 64), I96 / 4), ("post_s3", (64, 96), I96 * I3 / 4),
    ("post_v3", (0, 96), 0.25 / float(np.sqrt(128.0))),
    ("post_v3", (96, 128), 0.25 / 16.0),
    ("sc_s3", (0, 64), I8), ("sc_v3", (0, 96), I32C),
]
LAYERS = {1: (16, 0.25, 192, 96, 66), 2: (8, 1.0 / float(np.sqrt(8.0)), 192, 96, 65),
          3: (64, I8, 224, 128, 96)}


class Signal:

    def __init__(self, sem, unit=1, credit=2):
        self.sem, self.unit, self.count, self.credit = sem, unit, credit, credit

    def after(self, n):
        return (n + self.count) * self.unit

    def passed(self, n):
        self.count += n


class Step:

    def __init__(self, g, k, half):
        self.g, self.slot, self.quad, self.half = g, k % 2, k % 4, half


def pipeline(eng, chunks, stages):
    most = max(d for _, d in stages)
    lead = most + (-most) % 4
    rounds = (chunks - lead) // 4

    def static(t):
        for stage, d in stages:
            if 0 <= t - d < chunks:
                stage(Step(t - d, t - d, (t - d) // 2))

    for t in range(lead):
        static(t)
    with eng.Fori(0, rounds) as i:
        for k in range(4):
            for stage, d in stages:
                c = lead + k - d
                stage(Step(i * 4 + c, c, i * 2 + c // 2))
    for t in range(lead + 4 * rounds, chunks + most):
        static(t)


def ahead(g, k, chunks):
    return min(g + k, chunks) if type(g) is int else g + k


def gnn_kernel(nc, inp, out):
    nodes = inp["x"].shape[0]
    chunks = nodes // CHUNK
    tiles = chunks * TILES
    fix_rows = tiles // FIX_BLOCKS
    ctx = ExitStack()

    def sb(name, shape, dt=F32, own=None):
        return (own or ctx).enter_context(nc.sbuf_tensor(name, shape, dt))

    def two(name, shape, dt=F32, own=None):
        return [sb(f"{name}_{k}", shape, dt, own) for k in range(2)]

    def four(name, shape):
        return [sb(f"{name}_{k}", shape) for k in range(4)]

    def signal(name, unit=1, credit=96):
        s = Signal(ctx.enter_context(nc.semaphore(name)), unit, credit)
        signals.append(s)
        return s

    def slots(name, unit, credit=2):
        return [signal(f"{name}_{k}", unit, credit) for k in range(2)]

    def dram(name, shape, dt=F32):
        return nc.dram_tensor(name, shape, dt).ap()

    signals = []
    with ctx:
        src_table, dst_table = dram("src_table", [nodes, D]), dram("dst_table", [nodes, D])
        x_rows = [inp["x"]] + [dram(f"x_rows_{k}", [nodes, ROW]) for k in (1, 2, 3)]
        agg_dram = dram("agg_dram", [nodes, AGG])
        heads_dram, tails_dram = dram("heads_dram", [tiles, AGG]), dram("tails_dram", [tiles, AGG])
        sidx_dram = dram("sidx_dram", [chunks, P, TILES], I32)
        pen_dram = dram("pen_dram", [1, nodes + P])
        values_dram = dram("values_dram", [nodes, D])
        logit_dram, fmax_dram = dram("logit_dram", [HEADS, nodes]), dram("fmax_dram", [HEADS, nodes])

        w_all = sb("w_all", [P, WCOLS])

        def W(name, rows=None, cols=None):
            r, c = SHAPES[name]
            r0, r1 = rows or (0, r)
            c0, c1 = cols or (0, c)
            return w_all[r0:r1, OFFSETS[name] + c0:OFFSETS[name] + c1]

        ident = W("ident")
        power = sb("power", [P, 2 * TILES])
        half_pi = sb("half_pi", [P, 1])
        join_mask = sb("join_mask", [P, FIX_BLOCKS, tiles])
        join_idx = sb("join_idx", [P, FIX_BLOCKS], I32)

        idx = two("edge_idx", [P, 2 * TILES], I32)
        sidx = two("scatter_idx", [P, TILES], I32)
        dst_row = two("dst_row", [P, TILES, P], I32)
        attr = four("attr", [P, TILES, 6])
        scal_t = two("scal_t", [65, CHUNK])
        rows = four("rows", [P, TILES, ROW])
        agg = four("agg", [P, TILES, AGG])
        xs_t, xv_t = sb("xs_t", [65, CHUNK]), sb("xv_t", [96, CHUNK])
        hid_t = sb("hid_t", [65, CHUNK])
        e_ext = two("e_ext", [P, TILES, C0 + 5 * C1])
        radial = two("radial", [P, TILES, 224])
        seg = two("seg", [P, TILES, P])
        mid = two("mid", [P, TILES, 97 + 3 * P])
        mid_t = sb("mid_t", [P, 4, CHUNK])
        res = two("res", [P, TILES, AGG])
        tmp = [sb(f"tmp_{k}", [P, TILES * 96]) for k in range(4)]
        work, y = four("work", [P, TILES, D]), two("y", [P, TILES, D])
        aux = two("aux", [P, TILES, AGG])
        gate = two("gate", [P, TILES, 96])
        outs = two("outs", [P, TILES, ROW])
        stats = two("stats", [P, 96])
        gate_v = two("gate_v", [P, TILES, D])
        fm, bm = two("fm", [HEADS, CHUNK]), two("bm", [HEADS, CHUNK])
        hid2_t = sb("hid2_t", [65, CHUNK])
        psum = ctx.enter_context(nc.psum_tensor("banks", [P, 8, 512], F32))

        def bank(k, rows=P, cols=512):
            return psum[0:rows, k, 0:cols]

        def tiled(k, cols):
            return psum[:, k:k + 2, :].rearrange("p b (t c) -> p (b t) c", t=2)[:, :, 0:cols]

        ready = signal("ready", 1, 1)
        attr_in = slots("attr_in", 16)
        idx_in, sidx_in = slots("idx_in", 16), slots("sidx_in", 16)
        edge_in = slots("edge_in", 48)
        rows_in, rows_b_in = slots("rows_in", 64, 0), slots("rows_b_in", 64, 0)
        pre_in, table_out, hid_in, vec_in = (slots("pre_in", 16), slots("table_out", 32),
                                             slots("hid_in", 16), slots("vec_in", 32))
        scattered, ends_out = slots("scattered", 64, 0), slots("ends_out", 32)
        node_in, node_out = slots("node_in", 32), slots("node_out", 16)
        values_in, values_out = slots("values_in", 32), slots("values_out", 48)
        xt_mm, xt_sb = signal("xt_mm"), signal("xt_sb")
        hid_mm, hid_sb = signal("hid_mm"), signal("hid_sb")
        e_mm, e_sb = signal("e_mm"), signal("e_sb")
        w_mm, w_sb = signal("w_mm"), signal("w_sb")
        agg_mm, agg_sb = signal("agg_mm"), signal("agg_sb")
        post_mm, res_sb = signal("post_mm"), signal("res_sb")
        mid_step, pre_step, sum_step = signal("mid_step"), signal("pre_step"), signal("sum_step")
        scale_step, hidden_step = signal("scale_step"), signal("hidden_step")
        xt2_mm, xt2_sb = signal("xt2_mm"), signal("xt2_sb")
        sc_mm, gate_sb, hidden_mm = signal("sc_mm"), signal("gate_sb"), signal("hidden_mm")
        table_sb = signal("table_sb")
        root_sb, root2_sb = signal("root_sb"), signal("root2_sb")
        bias_sb, norm_sb = signal("bias_sb"), signal("norm_sb")
        logit_mm, logit_sb = signal("logit_mm"), signal("logit_sb")
        ht_mm, ht_sb = signal("ht_mm"), signal("ht_sb")
        h1_mm, h2_mm, h1t_mm, h2t_mm = signal("h1_mm"), signal("h2_mm"), signal("h1t_mm"), signal("h2t_mm")
        sq1_sb, sq2_sb, th1_sb, th2_sb = signal("sq1_sb"), signal("sq2_sb"), signal("th1_sb"), signal("th2_sb")
        h1t_sb, h2t_sb = signal("h1t_sb"), signal("h2t_sb")
        var1_step, var2_step, ln1_step, ln2_step = (signal("var1_step"), signal("var2_step"),
                                                    signal("ln1_step"), signal("ln2_step"))
        silu1_sb, silu2_sb = signal("silu1_sb"), signal("silu2_sb")
        alpha_mm, alpha_sb, leaky_step = signal("alpha_mm"), signal("alpha_sb"), signal("leaky_step")
        val_mm, val_sb, fmax_sb = signal("val_mm"), signal("val_sb"), signal("fmax_sb")
        setup_in, setup_step = signal("setup_in", 16, 1), signal("setup_step", 1, 1)
        setup_mm, setup_out = signal("setup_mm", 1, 1), signal("setup_out", 16, 1)
        agg_clear = signal("agg_clear", 16, 1)
        join_in, join_mm = signal("join_in", 16, 1), signal("join_mm", 1, 1)
        join_sum, join_out = signal("join_sum", 1, 1), signal("join_out", 16, 0)


        class Chain:

            def __init__(self, sig, g, per_chunk):
                self.sig, self.sem, self.n, self.per_chunk = sig, sig.sem, 0, per_chunk
                self.first = g * per_chunk

            def did(self, _):
                self.n += 1
                return self.n

            def after(self, n):
                return self.sig.after(self.first + n)

            def end(self):
                assert self.n == self.per_chunk, (self.n, self.per_chunk)

        def spread(ap, axis, shape):
            return ap.unsqueeze(axis).broadcast_to(shape)

        def precompute(eng, *values):
            for v in values:
                if type(v) is not int:
                    eng.compute_val(v)

        def load_dst_row(sp, slot, chunk):
            return sp.dma_start(
                dst_row[slot][:].rearrange("p t e -> p (t e)"),
                inp["dst_flat"][0, bass.ds(chunk * CHUNK, CHUNK)].partition_broadcast(P))

        def load_sidx(sp, s, chunk):
            precompute(sp, scattered[s.slot].after(s.half))
            sp.wait_ge(ready.sem, 1)
            sp.wait_ge(scattered[s.slot].sem, scattered[s.slot].after(s.half))
            sp.dma_start(sidx[s.slot][:], sidx_dram[bass.ds(chunk, 1)].rearrange("o p t -> (o p) t")) \
                .then_inc(sidx_in[s.slot].sem, 16)

        def store_ends(sp, s, chunk):
            precompute(sp, res_sb.after(s.g + 1))
            sp.wait_ge(ready.sem, 1)
            sp.wait_ge(res_sb.sem, res_sb.after(s.g + 1))
            for edge, table in ((0, heads_dram), (P - 1, tails_dram)):
                sp.dma_start(table[bass.ds(chunk * TILES, TILES), :].rearrange("(o t) c -> o t c", o=1),
                             res[s.slot][edge:edge + 1]).then_inc(ends_out[s.slot].sem, 16)

        def scatter(pool, s):
            precompute(pool, res_sb.after(s.g + 1), sidx_in[s.slot].after(s.half + 1))
            pool.wait_ge(ready.sem, 1)
            pool.wait_ge(res_sb.sem, res_sb.after(s.g + 1))
            pool.wait_ge(sidx_in[s.slot].sem, sidx_in[s.slot].after(s.half + 1))
            for t in range(TILES):
                pool.indirect_dma_start(
                    agg_dram, bass.IndirectOffsetOnAxis(sidx[s.slot][:, t:t + 1], 0),
                    res[s.slot][:, t, :], None, bounds_check=nodes - 1, oob_is_err=False,
                ).then_inc(scattered[s.slot].sem, 16)

        def segment_matrix(dve, slot, chain):
            return chain.did(dve.tensor_tensor(
                seg[slot][:], dst_row[slot][:],
                spread(idx[slot][:, TILES:], 2, [P, TILES, P]), ALU.is_equal).then_inc(chain.sem, 1))

        def messages(dve, slot, chain, e, w, attr6, with_scalar, crossed):
            es = e[:, :, 0:C0]
            ev = e[:, :, C0:].rearrange("p t (i c) -> p t i c", i=5)
            m = mid[slot]
            mv = m[:, :, 97:].rearrange("p t (i c) -> p t i c", i=3)
            e0, e1 = attr6[:, :, 0:1], attr6[:, :, 1:6]
            four = [P, TILES, 3, C1]

            def view(k, n=3 * C1):
                return tmp[k][:, 0:TILES * n].rearrange("p (t c) -> p t c", t=TILES)

            def view3(k):
                return tmp[k][:].rearrange("p (t i c) -> p t i c", t=TILES, i=3)

            def part(a, b):
                return spread(w[:, :, a:b], 2, four)

            outer = chain.did(dve.tensor_tensor(view(0, C0), w[:, :, 64:128], es, ALU.mult).then_inc(chain.sem, 1))
            dot = chain.did(dve.tensor_tensor(view3(1), ev[:, :, 0:3], spread(e1[:, :, 0:3], 3, four), ALU.mult).then_inc(chain.sem, 1))
            if with_scalar:
                s0 = chain.did(dve.tensor_tensor(view(2, C0), es, e0.broadcast_to([P, TILES, C0]), ALU.mult).then_inc(chain.sem, 1))
                v0 = chain.did(dve.tensor_tensor(view3(3), ev[:, :, 0:3], spread(e0, 3, four), ALU.mult).then_inc(chain.sem, 1))
            dve.wait_ge(chain.sem, chain.after(dot))
            dot = chain.did(dve.tensor_tensor(view3(1)[:, :, 0], view3(1)[:, :, 0], view3(1)[:, :, 1], ALU.add).then_inc(chain.sem, 1))
            if with_scalar:
                dve.wait_ge(chain.sem, chain.after(s0))
                chain.did(dve.tensor_tensor(m[:, :, 0:C0], w[:, :, 0:64], view(2, C0), ALU.mult).then_inc(chain.sem, 1))
                dve.wait_ge(chain.sem, chain.after(v0))
                v3 = chain.did(dve.tensor_tensor(mv[:, :, :, 64:96], part(128, 160), view3(3), ALU.mult).then_inc(chain.sem, 1))
            else:
                chain.did(dve.tensor_tensor(m[:, :, 0:C0], w[:, :, 0:64], es, ALU.mult).then_inc(chain.sem, 1))
                v3 = chain.did(dve.tensor_tensor(mv[:, :, :, 64:96], part(128, 160), ev[:, :, 0:3], ALU.mult).then_inc(chain.sem, 1))
            dve.wait_ge(chain.sem, chain.after(dot))
            dot = chain.did(dve.tensor_tensor(view3(1)[:, :, 0], view3(1)[:, :, 0], view3(1)[:, :, 2], ALU.add).then_inc(chain.sem, 1))
            dve.wait_ge(chain.sem, chain.after(outer))
            chain.did(dve.tensor_tensor(
                mv[:, :, :, 0:64], spread(view(0, C0), 2, [P, TILES, 3, C0]),
                spread(e1[:, :, 0:3], 3, [P, TILES, 3, C0]), ALU.mult).then_inc(chain.sem, 1))
            dve.wait_ge(chain.sem, chain.after(dot))
            last = chain.did(dve.tensor_tensor(m[:, :, 64:96], w[:, :, 160:192], view3(1)[:, :, 0], ALU.mult).then_inc(chain.sem, 1))
            if crossed:
                dve.wait_ge(chain.sem, chain.after(max(last, v3)))
                a = chain.did(dve.tensor_tensor(view3(2), ev[:, :, 1:4], spread(e1[:, :, 2:5], 3, four), ALU.mult).then_inc(chain.sem, 1))
                b = chain.did(dve.tensor_tensor(view3(3), ev[:, :, 2:5], spread(e1[:, :, 1:4], 3, four), ALU.mult).then_inc(chain.sem, 1))
                dve.wait_ge(chain.sem, chain.after(b))
                c = chain.did(dve.tensor_tensor(view3(2), view3(2), view3(3), ALU.subtract).then_inc(chain.sem, 1))
                dve.wait_ge(chain.sem, chain.after(c))
                chain.did(dve.tensor_tensor(mv[:, :, :, 96:128], part(192, 224), view3(2), ALU.mult).then_inc(chain.sem, 1))

        def edge_layer(layer):
            fan, radial_scale, w_cols, v_rows, s_cols = LAYERS[layer]
            crossed = layer == 3
            table, scalars = x_rows[layer], inp[f"scal_{layer}"]
            s_rows = SHAPES[f"post_s{layer}"][0]
            steps = 10 + 4 * crossed
            with nc.Block() as block:
                @block.sync
                def _(sp):
                    def load_edges(s):
                        precompute(sp, pre_step.after((s.g - 1) * 2))
                        sp.wait_ge(ready.sem, 1)
                        sp.wait_ge(pre_step.sem, pre_step.after((s.g - 1) * 2))
                        sp.dma_start(idx[s.slot][:], inp["edge_idx"][bass.ds(s.g, 1)].rearrange("o p t -> (o p) t")) \
                            .then_inc(idx_in[s.slot].sem, 16)
                        precompute(sp, hid_mm.after(s.g - 1), mid_step.after((s.g - 1) * steps))
                        sp.wait_ge(ready.sem, 1)
                        sp.wait_ge(hid_mm.sem, hid_mm.after(s.g - 1))
                        sp.wait_ge(mid_step.sem, mid_step.after((s.g - 1) * steps))
                        load_dst_row(sp, s.slot, s.g).then_inc(edge_in[s.slot].sem, 16)
                        sp.dma_start(attr[s.slot][:], inp["attr4"][bass.ds(s.g * CHUNK, CHUNK), :]
                                     .rearrange("(t p) c -> p t c", p=P)).then_inc(edge_in[s.slot].sem, 16)
                        sp.dma_start(scal_t[s.slot][0:fan, :], scalars[0:fan, bass.ds(s.g * CHUNK, CHUNK)]) \
                            .then_inc(edge_in[s.slot].sem, 16)

                    pipeline(sp, chunks, [
                        (load_edges, 0),
                        (lambda s: load_sidx(sp, s, s.g), 2), (lambda s: store_ends(sp, s, s.g), 3)])
                    for k in range(2):
                        sp.wait_ge(ends_out[k].sem, ends_out[k].after(chunks // 2))
                        sp.wait_ge(sidx_in[k].sem, sidx_in[k].after(chunks // 2))

                @block.gpsimd
                def _(pool):
                    def gather(s):
                        precompute(pool, idx_in[s.slot].after(s.half + 1), xt_mm.after(s.g - 1), pre_step.after((s.g - 1) * 2))
                        pool.wait_ge(ready.sem, 1)
                        pool.wait_ge(idx_in[s.slot].sem, idx_in[s.slot].after(s.half + 1))
                        pool.wait_ge(xt_mm.sem, xt_mm.after(s.g - 1))
                        pool.wait_ge(pre_step.sem, pre_step.after((s.g - 1) * 2))
                        for t in range(TILES):
                            pool.indirect_dma_start(
                                rows[s.slot][:, t, :], None, table,
                                bass.IndirectOffsetOnAxis(idx[s.slot][:, t:t + 1], 0),
                            ).then_inc(rows_in[s.slot].sem, 16)

                    pipeline(pool, chunks, [(gather, 0), (lambda s: scatter(pool, s), 3)])
                    for k in range(2):
                        pool.wait_ge(scattered[k].sem, scattered[k].after(chunks // 2))

                @block.tensor
                def _(pe):
                    def turn(s):
                        precompute(pe, rows_in[s.slot].after(s.half + 1), xt_sb.after(s.g))
                        pe.wait_ge(ready.sem, 1)
                        pe.wait_ge(rows_in[s.slot].sem, rows_in[s.slot].after(s.half + 1))
                        pe.wait_ge(xt_sb.sem, xt_sb.after(s.g))
                        for t in range(TILES):
                            pe.transpose(psum[0:C0, 0, t * P:(t + 1) * P], rows[s.slot][:, t, 0:C0], ident)
                        for t in range(TILES):
                            last = pe.transpose(psum[0:96, 1, t * P:(t + 1) * P], rows[s.slot][:, t, C0:D], ident)
                        last.then_inc(xt_mm.sem, 1)
                        precompute(pe, edge_in[s.slot].after(s.half + 1), res_sb.after(s.g - 2))
                        pe.wait_ge(ready.sem, 1)
                        pe.wait_ge(edge_in[s.slot].sem, edge_in[s.slot].after(s.half + 1))
                        pe.wait_ge(res_sb.sem, res_sb.after(s.g - 2))
                        pe.matmul(bank(6, 64), W(f"fc1_{layer}"), scal_t[s.slot][0:fan, :],
                                  start=True, stop=True).then_inc(hid_mm.sem, 1)

                    def linear(s):
                        pe.wait_ge(xt_sb.sem, xt_sb.after(s.g + 1))
                        pe.wait_ge(e_sb.sem, e_sb.after(s.g))
                        e_ps = tiled(2, D)
                        for t in range(TILES):
                            pe.matmul(e_ps[:, t, 0:C0], xs_t[0:C0, t * P:(t + 1) * P], W(f"e_s{layer}"),
                                      start=True, stop=True)
                            last = pe.matmul(e_ps[:, t, C0:D], xv_t[:, t * P:(t + 1) * P], W(f"e_v{layer}"),
                                             start=True, stop=True)
                        last.then_inc(e_mm.sem, 1)

                    def weights(s):
                        pe.wait_ge(hid_sb.sem, hid_sb.after(s.g + 1))
                        pe.wait_ge(w_sb.sem, w_sb.after(s.g))
                        w_ps = tiled(4, w_cols)
                        for t in range(TILES):
                            last = pe.matmul(w_ps[:, t], hid_t[0:64, t * P:(t + 1) * P], W(f"fc2_{layer}"),
                                             start=True, stop=True)
                        last.then_inc(w_mm.sem, 1)

                    def sums(s):
                        pe.wait_ge(mid_step.sem, mid_step.after((s.g + 1) * steps))
                        pe.wait_ge(hid_sb.sem, hid_sb.after(ahead(s.g, 3, chunks)))
                        pe.wait_ge(res_sb.sem, res_sb.after(s.g))
                        for k in range(4):
                            if k >= 2:
                                pe.wait_ge(agg_sb.sem, agg_sb.after(4 * s.g + k - 1))
                            n = s_rows if k == 0 else v_rows
                            at = 0 if k == 0 else 97 + P * (k - 1)
                            for t in range(TILES):
                                last = pe.matmul(psum[0:n, 6 + k % 2, t * P:(t + 1) * P],
                                                 mid[s.slot][:, t, at:at + n], seg[s.slot][:, t, :],
                                                 start=True, stop=True)
                            last.then_inc(agg_mm.sem, 1)

                    def second(s):
                        pe.wait_ge(agg_sb.sem, agg_sb.after(4 * s.g + 4))
                        post = tiled(6, 2 * 96)
                        for t in range(TILES):
                            cut = slice(t * P, (t + 1) * P)
                            pe.matmul(post[:, t, 0:s_cols], mid_t[0:s_rows, 0, cut], W(f"post_s{layer}"),
                                      start=True, stop=True)
                            for i in range(3):
                                last = pe.matmul(post[:, t, 96 + 32 * i:128 + 32 * i],
                                                 mid_t[0:v_rows, 1 + i, cut], W(f"post_v{layer}"),
                                                 start=True, stop=True)
                        last.then_inc(post_mm.sem, 1)

                    pipeline(pe, chunks, [(turn, 0), (sums, 2), (linear, 0), (weights, 0), (second, 2)])

                @block.scalar
                def _(act):
                    def turned(s):
                        act.wait_ge(xt_mm.sem, xt_mm.after(s.g + 1))
                        act.wait_ge(e_mm.sem, e_mm.after(s.g))
                        act.activation(xs_t[0:C0, :], bank(0, C0), ACT.Copy)
                        act.activation(xv_t[:, :], bank(1, 96), ACT.Copy).then_inc(xt_sb.sem, 1)
                        act.wait_ge(hid_mm.sem, hid_mm.after(s.g + 1))
                        act.wait_ge(w_mm.sem, w_mm.after(s.g))
                        act.activation(hid_t[0:64, :], bank(6, 64), ACT.Silu, scale=radial_scale) \
                            .then_inc(hid_sb.sem, 1)

                    def linear(s):
                        act.wait_ge(e_mm.sem, e_mm.after(s.g + 1))
                        act.wait_ge(mid_step.sem, mid_step.after((s.g - 1) * steps))
                        e_ps = tiled(2, D)
                        act.activation(e_ext[s.slot][:, :, 0:D], e_ps, ACT.Copy)
                        act.activation(e_ext[s.slot][:, :, D:], e_ps[:, :, C0:C0 + 64], ACT.Copy) \
                            .then_inc(e_sb.sem, 1)
                        act.wait_ge(w_mm.sem, w_mm.after(s.g + 1))
                        act.activation(radial[s.slot][:, :, 0:w_cols], tiled(4, w_cols), ACT.Copy) \
                            .then_inc(w_sb.sem, 1)

                    def sums(s):
                        act.wait_ge(post_mm.sem, post_mm.after(s.g))
                        for k in range(4):
                            n = s_rows if k == 0 else v_rows
                            act.wait_ge(agg_mm.sem, agg_mm.after(4 * s.g + k + 1))
                            act.activation(mid_t[0:n, k, :], bank(6 + k % 2, n), ACT.Copy) \
                                .then_inc(agg_sb.sem, 1)

                    def second(s):
                        act.wait_ge(post_mm.sem, post_mm.after(s.g + 1))
                        act.wait_ge(scattered[s.slot].sem, scattered[s.slot].after(s.half))
                        act.wait_ge(ends_out[s.slot].sem, ends_out[s.slot].after(s.half))
                        post = tiled(6, 2 * 96)
                        v_out = C0 if layer < 3 else 96
                        act.activation(res[s.slot][:, :, 0:v_out], post[:, :, 0:v_out], ACT.Copy)
                        if layer < 3:
                            act.activation(res[s.slot][:, :, D:D + s_cols - C0], post[:, :, C0:s_cols], ACT.Copy)
                        act.activation(
                            res[s.slot][:, :, v_out:v_out + 96].rearrange("p t (c i) -> p t i c", i=3),
                            post[:, :, 96:192].rearrange("p t (i c) -> p t i c", i=3), ACT.Copy) \
                            .then_inc(res_sb.sem, 1)

                    pipeline(act, chunks, [(turned, 0), (sums, 2), (linear, 0), (second, 2)])

                @block.vector
                def _(dve):
                    def prepare(s):
                        chain = Chain(pre_step, s.g, 2)
                        dve.wait_ge(chain.sem, chain.after(0))
                        dve.wait_ge(edge_in[s.slot].sem, edge_in[s.slot].after(s.half + 1))
                        dve.wait_ge(idx_in[s.slot].sem, idx_in[s.slot].after(s.half + 1))
                        dve.wait_ge(agg_mm.sem, agg_mm.after(4 * (s.g - 1)))
                        segment_matrix(dve, s.slot, chain)
                        dve.wait_ge(rows_in[s.slot].sem, rows_in[s.slot].after(s.half + 1))
                        chain.did(dve.tensor_tensor(
                            attr[s.slot][:], attr[s.slot][:],
                            rows[s.slot][:, :, D:ROW].broadcast_to([P, TILES, 6]), ALU.mult).then_inc(chain.sem, 1))
                        chain.end()

                    def message(s):
                        chain = Chain(mid_step, s.g, steps)
                        dve.wait_ge(chain.sem, chain.after(0))
                        dve.wait_ge(pre_step.sem, pre_step.after((s.g + 1) * 2))
                        dve.wait_ge(e_sb.sem, e_sb.after(s.g + 1))
                        dve.wait_ge(w_sb.sem, w_sb.after(s.g + 1))
                        dve.wait_ge(agg_mm.sem, agg_mm.after(4 * (s.g - 1)))
                        messages(dve, s.slot, chain, e_ext[s.slot], radial[s.slot], attr[s.slot], True, crossed)
                        chain.end()

                    pipeline(dve, chunks, [(message, 1), (prepare, 0)])
            for sig in (xt_mm, xt_sb, hid_mm, hid_sb, e_mm, e_sb, w_mm, w_sb, post_mm, res_sb):
                sig.passed(chunks)
            for sig in (*idx_in, *edge_in, *rows_in, *sidx_in, *scattered, *ends_out):
                sig.passed(chunks // 2)
            for sig in (agg_mm, agg_sb):
                sig.passed(4 * chunks)
            mid_step.passed(steps * chunks)
            pre_step.passed(2 * chunks)

        def join(layer):
            with ExitStack() as own, nc.Block() as block:
                join_h, join_t, join_o = (sb(f"join_{n}_{layer}", [P, FIX_BLOCKS, AGG], own=own)
                                          for n in ("heads", "tails", "sums"))

                @block.sync
                def _(sp):
                    for table, to in ((heads_dram, join_h), (tails_dram, join_t)):
                        sp.dma_start(to[0:fix_rows], table.rearrange("(b p) c -> p b c", p=fix_rows)) \
                            .then_inc(join_in.sem, 16)

                @block.tensor
                def _(pe):
                    pe.wait_ge(join_in.sem, join_in.after(2))
                    sums = tiled(0, AGG)
                    for b in range(FIX_BLOCKS):
                        for a in range(b + 1):
                            last = pe.matmul(sums[0:fix_rows, b, :],
                                             join_mask[0:fix_rows, a, b * fix_rows:(b + 1) * fix_rows],
                                             join_t[0:fix_rows, a, :], start=(a == 0), stop=(a == b))
                    last.then_inc(join_mm.sem, 1)

                @block.vector
                def _(dve):
                    dve.wait_ge(join_in.sem, join_in.after(2))
                    dve.wait_ge(join_mm.sem, join_mm.after(1))
                    dve.tensor_tensor(join_o[0:fix_rows], tiled(0, AGG)[0:fix_rows], join_h[0:fix_rows],
                                      ALU.add).then_inc(join_sum.sem, 1)

                @block.gpsimd
                def _(pool):
                    pool.wait_ge(join_sum.sem, join_sum.after(1))
                    for b in range(FIX_BLOCKS):
                        pool.indirect_dma_start(
                            agg_dram, bass.IndirectOffsetOnAxis(join_idx[0:fix_rows, b:b + 1], 0),
                            join_o[0:fix_rows, b, :], None, bounds_check=nodes - 1, oob_is_err=False,
                        ).then_inc(join_out.sem, 16)
                    pool.wait_ge(join_out.sem, join_out.after(FIX_BLOCKS))
            join_in.passed(2)
            join_mm.passed(1)
            join_sum.passed(1)
            join_out.passed(FIX_BLOCKS)

        def load_nodes(sp, s, table, done, steps, pre_steps):
            precompute(sp, done.after((s.g - 3) * steps), pre_step.after((s.g - 1) * pre_steps))
            sp.wait_ge(ready.sem, 1)
            sp.wait_ge(done.sem, done.after((s.g - 3) * steps))
            sp.wait_ge(pre_step.sem, pre_step.after((s.g - 1) * pre_steps))
            nodes_of = table[bass.ds(s.g * CHUNK, CHUNK), :].rearrange("(p t) c -> p t c", t=TILES)
            sp.dma_start(rows[s.quad][:], nodes_of).then_inc(node_in[s.slot].sem, 16)
            sp.dma_start(agg[s.quad][:], agg_dram[bass.ds(s.g * CHUNK, CHUNK), :]
                         .rearrange("(p t) c -> p t c", t=TILES)).then_inc(node_in[s.slot].sem, 16)

        def store_nodes(sp, s, table):
            precompute(sp, norm_sb.after(s.g + 1))
            sp.wait_ge(ready.sem, 1)
            sp.wait_ge(norm_sb.sem, norm_sb.after(s.g + 1))
            sp.dma_start(table[bass.ds(s.g * CHUNK, CHUNK), :].rearrange("(p t) c -> p t c", t=TILES),
                         outs[s.slot][:]).then_inc(node_out[s.slot].sem, 16)

        def transpose_rows(pe, ap, s_cols, v_at, banks):
            for t in range(TILES):
                pe.transpose(psum[0:s_cols, banks, t * P:(t + 1) * P], ap[:, t, 0:s_cols], ident)
            for t in range(TILES):
                last = pe.transpose(psum[0:96, banks + 1, t * P:(t + 1) * P], ap[:, t, v_at:v_at + 96], ident)
            return last

        def mean_var(dve, chain, st, source, at):
            need = [chain.did(dve.bn_stats(st[:, 6 * t:6 * t + 6], source[:, t, :]).then_inc(chain.sem, 1)) for t in range(TILES)]
            for t in range(TILES):
                precompute(dve, chain.after(need[t]))
                dve.wait_ge(ready.sem, 1)
                dve.wait_ge(chain.sem, chain.after(need[t]))
                last = chain.did(dve.bn_aggr(st[:, at + 2 * t:at + 2 * t + 2], st[:, 6 * t:6 * t + 6]).then_inc(chain.sem, 1))
            return last

        def pairs(st, at, which):
            return st[:, at:at + 2 * TILES].rearrange("p (t k) -> p t k", k=2)[:, :, which]

        def final_sums(dve, s, chain):
            st = stats[s.slot]
            last = mean_var(dve, chain, st, y[s.slot], 24)
            dve.wait_ge(chain.sem, chain.after(last))
            chain.did(dve.tensor_scalar(st[:, 32:36], pairs(st, 24, 1), 1e-5, None, ALU.add).then_inc(chain.sem, 1))
            dve.wait_ge(node_out[s.slot].sem, node_out[s.slot].after(s.half))
            chain.did(dve.tensor_copy(outs[s.slot][:, :, D:ROW], rows[s.quad][:, :, D:ROW]).then_inc(chain.sem, 1))

        def root(pool, s, at, n, done, steps, sig):
            precompute(pool, done.after((s.g + 1) * steps))
            pool.wait_ge(ready.sem, 1)
            pool.wait_ge(done.sem, done.after((s.g + 1) * steps))
            st = stats[s.slot]
            pool.tensor_tensor(st[:, at + n:at + 2 * n], st[:, at:at + n], power[:, 0:n], ALU.pow) \
                .then_inc(sig.sem, 1)

        def final_bias(dve, s):
            st = stats[s.slot]
            dve.wait_ge(root2_sb.sem, root2_sb.after(s.g + 1))
            dve.scalar_tensor_tensor(st[:, 40:44], pairs(st, 24, 0), -1.0, st[:, 36:40], ALU.mult, ALU.mult) \
                .then_inc(bias_sb.sem, 1)

        def final_norm(act, s):
            st = stats[s.slot]
            act.wait_ge(bias_sb.sem, bias_sb.after(s.g + 1))
            for t in range(TILES):
                last = act.activation(outs[s.slot][:, t, 0:D], y[s.slot][:, t, :], ACT.Identity,
                                      bias=st[:, 40 + t:41 + t], scale=st[:, 36 + t:37 + t])
            last.then_inc(norm_sb.sem, 1)

        def node_layer(layer):
            table = x_rows[layer]
            to = x_rows[layer + 1] if layer < 3 else out
            sc_cols = 64 if layer < 3 else 96
            pre_steps = {1: 4, 2: 9, 3: 2}[layer]
            sum_steps = {1: 9, 2: 10, 3: 4}[layer] + 2 * TILES + 2
            coef = 48
            with nc.Block() as block:
                @block.sync
                def _(sp):
                    pipeline(sp, chunks, [
                        (lambda s: load_nodes(sp, s, table, sum_step, sum_steps, pre_steps), 0),
                        (lambda s: store_nodes(sp, s, to), 3)])
                    for k in range(2):
                        sp.wait_ge(node_out[k].sem, node_out[k].after(chunks // 2))

                @block.tensor
                def _(pe):
                    def front(s):
                        precompute(pe, node_in[s.slot].after(s.half + 1), xt_sb.after(s.g))
                        pe.wait_ge(ready.sem, 1)
                        pe.wait_ge(node_in[s.slot].sem, node_in[s.slot].after(s.half + 1))
                        pe.wait_ge(xt_sb.sem, xt_sb.after(s.g))
                        transpose_rows(pe, rows[s.quad], C0, C0, 0).then_inc(xt_mm.sem, 1)

                    def back(s):
                        pe.wait_ge(xt_sb.sem, xt_sb.after(s.g + 1))
                        pe.wait_ge(sum_step.sem, sum_step.after((s.g - 1) * sum_steps))
                        pe.wait_ge(pre_step.sem, pre_step.after((s.g - 1) * pre_steps))
                        sc = tiled(2 + 2 * s.slot, sc_cols + 96)
                        for t in range(TILES):
                            cut = slice(t * P, (t + 1) * P)
                            pe.matmul(sc[:, t, 0:sc_cols], xs_t[0:C0, cut], W(f"sc_s{layer}"), start=True, stop=True)
                            last = pe.matmul(sc[:, t, sc_cols:], xv_t[:, cut], W(f"sc_v{layer}"), start=True, stop=True)
                        last.then_inc(sc_mm.sem, 1)

                    pipeline(pe, chunks, [(front, 0), (back, 0)])

                @block.scalar
                def _(act):
                    def front(s):
                        act.wait_ge(xt_mm.sem, xt_mm.after(s.g + 1))
                        act.wait_ge(sc_mm.sem, sc_mm.after(s.g))
                        act.activation(xs_t[0:C0, :], bank(0, C0), ACT.Copy)
                        act.activation(xv_t[:, :], bank(1, 96), ACT.Copy).then_inc(xt_sb.sem, 1)

                    def gates(s):
                        st = stats[s.slot]
                        act.wait_ge(pre_step.sem, pre_step.after((s.g + 1) * pre_steps))
                        act.wait_ge(sum_step.sem, sum_step.after((s.g - 1) * sum_steps))
                        if layer == 2:
                            act.activation(st[:, 60:64], st[:, 52:56], ACT.Sin)
                            act.activation(st[:, 64:68], st[:, 56:60], ACT.Sin, bias=half_pi[:, 0:1], scale=-1.0) \
                                .then_inc(gate_sb.sem, 1)
                        else:
                            act.activation(gate[s.slot][:, :, 0:64], aux[s.slot][:, :, 0:64], ACT.Silu)
                            act.activation(gate[s.slot][:, :, 64:96], aux[s.slot][:, :, 64:96], ACT.Tanh, scale=0.5) \
                                .then_inc(gate_sb.sem, 1)

                    stages = [(front, 0), (lambda s: final_norm(act, s), 2)]
                    if layer > 1:
                        stages.insert(1, (gates, 0))
                    pipeline(act, chunks, stages)

                @block.gpsimd
                def _(pool):
                    pipeline(pool, chunks, [
                        (lambda s: root(pool, s, 32, TILES, sum_step, sum_steps, root2_sb), 0)])

                @block.vector
                def _(dve):
                    def before(s):
                        chain = Chain(pre_step, s.g, pre_steps)
                        dve.wait_ge(chain.sem, chain.after(0))
                        st, sums, attrs = stats[s.slot], agg[s.quad], rows[s.quad][:, :, D]
                        dve.wait_ge(node_in[s.slot].sem, node_in[s.slot].after(s.half + 1))
                        dve.wait_ge(sum_step.sem, sum_step.after((s.g - 1) * sum_steps))
                        if layer == 1:
                            k = chain.did(dve.tensor_scalar(st[:, 52:56], sums[:, :, D + 1], 1.0, None, ALU.max).then_inc(chain.sem, 1))
                            dve.wait_ge(chain.sem, chain.after(k))
                            k = chain.did(dve.reciprocal(st[:, 56:60], st[:, 52:56]).then_inc(chain.sem, 1))
                            dve.wait_ge(chain.sem, chain.after(k))
                            k = chain.did(dve.tensor_tensor(st[:, 60:64], st[:, 56:60], attrs, ALU.mult).then_inc(chain.sem, 1))
                            dve.wait_ge(chain.sem, chain.after(k))
                            chain.did(dve.tensor_tensor(st[:, 64:68], sums[:, :, D], st[:, 60:64], ALU.mult).then_inc(chain.sem, 1))
                        elif layer == 2:
                            angle, r, turns = st[:, 68:72], st[:, 52:56], st[:, 72:76]
                            two_pi = 2 * np.pi
                            p1 = float(np.float32(6.28125))
                            p2 = float(np.float32(np.floor((two_pi - p1) * 2 ** 22) / 2 ** 22))
                            p3 = float(np.float32(two_pi - p1 - p2))
                            nearest = 1.5 * 2.0 ** 23
                            k = chain.did(dve.scalar_tensor_tensor(angle, sums[:, :, D], 0.1, attrs, ALU.mult, ALU.mult).then_inc(chain.sem, 1))
                            dve.wait_ge(chain.sem, chain.after(k))
                            k = chain.did(dve.tensor_scalar(turns, angle, 1 / two_pi, nearest, ALU.mult, ALU.add).then_inc(chain.sem, 1))
                            dve.wait_ge(chain.sem, chain.after(k))
                            k = chain.did(dve.tensor_scalar(turns, turns, nearest, None, ALU.subtract).then_inc(chain.sem, 1))
                            dve.wait_ge(chain.sem, chain.after(k))
                            k = chain.did(dve.scalar_tensor_tensor(r, turns, -p1, angle, ALU.mult, ALU.add).then_inc(chain.sem, 1))
                            dve.wait_ge(chain.sem, chain.after(k))
                            k = chain.did(dve.scalar_tensor_tensor(r, turns, -p2, r, ALU.mult, ALU.add).then_inc(chain.sem, 1))
                            dve.wait_ge(chain.sem, chain.after(k))
                            k = chain.did(dve.scalar_tensor_tensor(r, turns, -p3, r, ALU.mult, ALU.add).then_inc(chain.sem, 1))
                            dve.wait_ge(chain.sem, chain.after(k))
                            k = chain.did(dve.tensor_scalar(r, r, 3.1415925, -3.1415925, ALU.min, ALU.max).then_inc(chain.sem, 1))
                            dve.wait_ge(chain.sem, chain.after(k))
                            k = chain.did(dve.tensor_scalar(angle, r, -1.0, None, ALU.mult).then_inc(chain.sem, 1))
                            dve.wait_ge(chain.sem, chain.after(k))
                            chain.did(dve.tensor_tensor(st[:, 56:60], r, angle, ALU.max).then_inc(chain.sem, 1))
                        else:
                            dve.wait_ge(sc_mm.sem, sc_mm.after(s.g + 1))
                            dve.wait_ge(gate_sb.sem, gate_sb.after(s.g - 1))
                            k = chain.did(dve.tensor_tensor(
                                aux[s.slot][:], tiled(2 + 2 * s.slot, AGG), sums[:], ALU.add).then_inc(chain.sem, 1))
                            dve.wait_ge(chain.sem, chain.after(k))
                            chain.did(dve.tensor_tensor(
                                aux[s.slot][:], aux[s.slot][:],
                                rows[s.quad][:, :, D:ROW].broadcast_to([P, TILES, AGG]), ALU.mult).then_inc(chain.sem, 1))
                        chain.end()

                    def combine(s):
                        chain = Chain(sum_step, s.g, sum_steps)
                        dve.wait_ge(chain.sem, chain.after(0))
                        st, x, sums = stats[s.slot], rows[s.quad], agg[s.quad]
                        attrs, yy = x[:, :, D], y[s.slot]
                        dve.wait_ge(pre_step.sem, pre_step.after((s.g + 1) * pre_steps))
                        dve.wait_ge(norm_sb.sem, norm_sb.after(s.g - 1))
                        if layer < 3:
                            sc = tiled(2 + 2 * s.slot, D)
                            dve.wait_ge(sc_mm.sem, sc_mm.after(s.g + 1))
                            if layer == 1:
                                k1, k2 = attrs, st[:, coef:coef + 4]
                                k = chain.did(dve.tensor_tensor(k2, st[:, 64:68], st[:, 60:64], ALU.mult).then_inc(chain.sem, 1))
                            else:
                                dve.wait_ge(gate_sb.sem, gate_sb.after(s.g + 1))
                                k1, k2 = st[:, 76:80], st[:, coef:coef + 4]
                                chain.did(dve.tensor_tensor(k1, st[:, 64:68], attrs, ALU.mult).then_inc(chain.sem, 1))
                                k = chain.did(dve.tensor_tensor(k2, st[:, 60:64], attrs, ALU.mult).then_inc(chain.sem, 1))
                            dve.wait_ge(chain.sem, chain.after(k))
                            one = [chain.did(dve.scalar_tensor_tensor(
                                yy[:, t, :], sc[:, t, :], x[:, t, D:ROW] if layer == 1 else k1[:, t:t + 1],
                                x[:, t, 0:D], ALU.mult, ALU.add).then_inc(chain.sem, 1)) for t in range(TILES)]
                            for t in range(TILES):
                                dve.wait_ge(chain.sem, chain.after(one[t]))
                                k = chain.did(dve.scalar_tensor_tensor(
                                    yy[:, t, :], sums[:, t, 0:D], k2[:, t:t + 1], yy[:, t, :], ALU.mult, ALU.add).then_inc(chain.sem, 1))
                        else:
                            dve.wait_ge(gate_sb.sem, gate_sb.after(s.g + 1))
                            g, z = gate[s.slot], aux[s.slot]
                            k = chain.did(dve.tensor_scalar(g[:, :, 64:96], g[:, :, 64:96], 0.5, 0.5, ALU.mult, ALU.add).then_inc(chain.sem, 1))
                            chain.did(dve.tensor_tensor(yy[:, :, 0:C0], g[:, :, 0:64], x[:, :, 0:C0], ALU.add).then_inc(chain.sem, 1))
                            dve.wait_ge(chain.sem, chain.after(k))
                            four = [P, TILES, C1, 3]
                            zv = z[:, :, 96:].rearrange("p t (c i) -> p t c i", i=3)
                            k = chain.did(dve.tensor_tensor(zv, zv, spread(g[:, :, 64:96], 3, four), ALU.mult).then_inc(chain.sem, 1))
                            dve.wait_ge(chain.sem, chain.after(k))
                            k = chain.did(dve.tensor_tensor(yy[:, :, C0:], z[:, :, 96:], x[:, :, C0:D], ALU.add).then_inc(chain.sem, 1))
                        dve.wait_ge(chain.sem, chain.after(k))
                        final_sums(dve, s, chain)
                        chain.end()

                    pipeline(dve, chunks, [(before, 0), (combine, 1), (lambda s: final_bias(dve, s), 2)])
            for sig in (xt_mm, xt_sb, sc_mm, root2_sb, bias_sb, norm_sb):
                sig.passed(chunks)
            if layer > 1:
                gate_sb.passed(chunks)
            for sig in (*node_in, *node_out):
                sig.passed(chunks // 2)
            pre_step.passed(pre_steps * chunks)
            sum_step.passed(sum_steps * chunks)

        def node_pre():
            pre_steps, scale_steps = 2 * TILES + 4, 2 * TILES
            with ExitStack() as own, nc.Block() as block:
                tables = two("tables", [P, 2, TILES, D], own=own)

                @block.sync
                def _(sp):
                    def load(s):
                        precompute(sp, scale_step.after((s.g - 3) * scale_steps), pre_step.after((s.g - 1) * pre_steps))
                        sp.wait_ge(ready.sem, 1)
                        sp.wait_ge(pre_step.sem, pre_step.after((s.g - 1) * pre_steps))
                        sp.wait_ge(scale_step.sem, scale_step.after((s.g - 3) * scale_steps))
                        sp.dma_start(rows[s.quad][:], x_rows[0][bass.ds(s.g * CHUNK, CHUNK), :]
                                     .rearrange("(p t) c -> p t c", t=TILES)).then_inc(pre_in[s.slot].sem, 16)

                    def store(s):
                        precompute(sp, table_sb.after(s.g + 1))
                        sp.wait_ge(ready.sem, 1)
                        sp.wait_ge(table_sb.sem, table_sb.after(s.g + 1))
                        for k, table in enumerate((src_table, dst_table)):
                            sp.dma_start(table[bass.ds(s.g * CHUNK, CHUNK), :].rearrange("(p t) c -> p t c", t=TILES),
                                         tables[s.slot][:, k]).then_inc(table_out[s.slot].sem, 16)

                    pipeline(sp, chunks, [(load, 0), (store, 2)])
                    for k in range(2):
                        sp.wait_ge(table_out[k].sem, table_out[k].after(chunks // 2))

                @block.vector
                def _(dve):
                    def statistics(s):
                        chain = Chain(pre_step, s.g, pre_steps)
                        dve.wait_ge(chain.sem, chain.after(0))
                        st, x = stats[s.slot], rows[s.quad]
                        dve.wait_ge(pre_in[s.slot].sem, pre_in[s.slot].after(s.half + 1))
                        dve.wait_ge(scale_step.sem, scale_step.after((s.g - 1) * scale_steps))
                        a = chain.did(dve.tensor_tensor(aux[s.slot][:, :, 0:96], x[:, :, C0:D], x[:, :, C0:D], ALU.mult).then_inc(chain.sem, 1))
                        b = mean_var(dve, chain, st, x[:, :, 0:C0], 24)
                        dve.wait_ge(chain.sem, chain.after(max(a, b)))
                        b = chain.did(dve.tensor_reduce(st[:, 48:52], aux[s.slot][:, :, 0:96], AX_X, ALU.add).then_inc(chain.sem, 1))
                        chain.did(dve.tensor_scalar(st[:, 32:36], pairs(st, 24, 1), 1e-5, None, ALU.add).then_inc(chain.sem, 1))
                        dve.wait_ge(chain.sem, chain.after(b))
                        chain.did(dve.tensor_scalar(st[:, 36:40], st[:, 48:52], 1.0 / 96, 1e-5, ALU.mult, ALU.add).then_inc(chain.sem, 1))
                        chain.end()

                    def scale(s):
                        chain = Chain(scale_step, s.g, scale_steps)
                        dve.wait_ge(chain.sem, chain.after(0))
                        st, x, n = stats[s.slot], rows[s.quad], work[s.quad]
                        dve.wait_ge(root_sb.sem, root_sb.after(s.g + 1))
                        dve.wait_ge(xt_mm.sem, xt_mm.after(s.g - 1))
                        for t in range(TILES):
                            chain.did(dve.tensor_scalar(
                                n[:, t, 0:C0], x[:, t, 0:C0], st[:, 24 + 2 * t:25 + 2 * t], st[:, 40 + t:41 + t],
                                ALU.subtract, ALU.mult).then_inc(chain.sem, 1))
                        for t in range(TILES):
                            chain.did(dve.tensor_scalar(
                                n[:, t, C0:], x[:, t, C0:D], st[:, 44 + t:45 + t], None, ALU.mult).then_inc(chain.sem, 1))
                        chain.end()

                    pipeline(dve, chunks, [(statistics, 0), (scale, 1)])

                @block.gpsimd
                def _(pool):
                    pipeline(pool, chunks, [
                        (lambda s: root(pool, s, 32, 2 * TILES, pre_step, pre_steps, root_sb), 0)])

                @block.tensor
                def _(pe):
                    def front(s):
                        precompute(pe, scale_step.after((s.g + 1) * scale_steps), xt_sb.after(s.g))
                        pe.wait_ge(ready.sem, 1)
                        pe.wait_ge(scale_step.sem, scale_step.after((s.g + 1) * scale_steps))
                        pe.wait_ge(xt_sb.sem, xt_sb.after(s.g))
                        transpose_rows(pe, work[s.quad], C0, C0, 0).then_inc(xt_mm.sem, 1)

                    def back(s):
                        pe.wait_ge(xt_sb.sem, xt_sb.after(s.g + 1))
                        pe.wait_ge(table_sb.sem, table_sb.after(s.g))
                        for t in range(TILES):
                            cut = slice(t * P, (t + 1) * P)
                            pe.matmul(psum[:, 2 + t, 0:128], xs_t[:, cut], W("sd_s"), start=True, stop=True)
                            last = pe.matmul(psum[:, 2 + t, 128:320], xv_t[:, cut], W("sd_v"), start=True, stop=True)
                        last.then_inc(sc_mm.sem, 1)

                    pipeline(pe, chunks, [(front, 0), (back, 0)])

                @block.scalar
                def _(act):
                    def front(s):
                        act.wait_ge(xt_mm.sem, xt_mm.after(s.g + 1))
                        act.wait_ge(sc_mm.sem, sc_mm.after(s.g))
                        act.activation(xs_t[0:C0, :], bank(0, C0), ACT.Copy)
                        act.activation(xv_t[:, :], bank(1, 96), ACT.Copy).then_inc(xt_sb.sem, 1)

                    def back(s):
                        act.wait_ge(sc_mm.sem, sc_mm.after(s.g + 1))
                        act.wait_ge(table_out[s.slot].sem, table_out[s.slot].after(s.half))
                        ps = psum[:, 2:6, :]
                        act.activation(tables[s.slot][:, :, :, 0:C0],
                                       ps[:, :, 0:128].rearrange("p t (k c) -> p k t c", k=2), ACT.Copy)
                        act.activation(tables[s.slot][:, :, :, C0:],
                                       ps[:, :, 128:320].rearrange("p t (k c) -> p k t c", k=2), ACT.Copy) \
                            .then_inc(table_sb.sem, 1)

                    pipeline(act, chunks, [(front, 0), (back, 0)])
            for sig in (xt_mm, xt_sb, sc_mm, table_sb, root_sb):
                sig.passed(chunks)
            for sig in (*pre_in, *table_out):
                sig.passed(chunks // 2)
            pre_step.passed(pre_steps * chunks)
            scale_step.passed(scale_steps * chunks)

        def edge_logits():
            steps = 2 + 8 + 4
            with ExitStack() as own, nc.Block() as block:
                sq, hn, hu, sq_b, hn_b, hu_b = (two(n, [P, TILES, 64], own=own)
                                                for n in ("sq", "hn", "hu", "sq_b", "hn_b", "hu_b"))
                h1_rows, h2_rows = two("h1_rows", [P, TILES, 64], own=own), two("h2_rows", [P, TILES, 64], own=own)
                vec_sq = two("vec_sq", [P, TILES, 3], own=own)
                alpha_t, leaky_t = sb("alpha_t", [64, CHUNK], own=own), sb("leaky_t", [64, CHUNK], own=own)
                pen, lg = two("pen", [HEADS, CHUNK], own=own), two("lg", [HEADS, CHUNK], own=own)

                @block.sync
                def _(sp):
                    def load_scalars(s):
                        precompute(sp, h1_mm.after(s.g - 1))
                        sp.wait_ge(ready.sem, 1)
                        sp.wait_ge(h1_mm.sem, h1_mm.after(s.g - 1))
                        sp.dma_start(scal_t[s.slot][:], inp["scal_3"][:, bass.ds(s.g * CHUNK, CHUNK)]) \
                            .then_inc(hid_in[s.slot].sem, 16)

                    def load_vectors(s):
                        precompute(sp, mid_step.after((s.g - 3) * steps), var2_step.after((s.g - 1) * 5))
                        sp.wait_ge(ready.sem, 1)
                        sp.wait_ge(mid_step.sem, mid_step.after((s.g - 3) * steps))
                        sp.wait_ge(var2_step.sem, var2_step.after((s.g - 1) * 5))
                        sp.dma_start(attr[s.quad][:], inp["vec"][bass.ds(s.g * CHUNK, CHUNK), :]
                                     .rearrange("(t p) c -> p t c", p=P)).then_inc(attr_in[s.slot].sem, 16)

                    def load_indices(s):
                        precompute(sp, mid_step.after((s.g - 1) * steps))
                        sp.wait_ge(ready.sem, 1)
                        sp.wait_ge(mid_step.sem, mid_step.after((s.g - 1) * steps))
                        sp.dma_start(idx[s.slot][:], inp["edge_idx"][bass.ds(s.g, 1)].rearrange("o p t -> (o p) t")) \
                            .then_inc(idx_in[s.slot].sem, 16)

                    def load_penalties(s):
                        precompute(sp, fmax_sb.after(s.g - 1))
                        sp.wait_ge(ready.sem, 1)
                        sp.wait_ge(fmax_sb.sem, fmax_sb.after(s.g - 1))
                        sp.dma_start(pen[s.slot][:], pen_dram[0, bass.ds(s.g * CHUNK, CHUNK)].partition_broadcast(HEADS)) \
                            .then_inc(pre_in[s.slot].sem, 16)

                    def clear(s):
                        sp.dma_start(agg_dram[bass.ds(s.g * CHUNK, CHUNK), :].rearrange("(p t) c -> p t c", t=TILES),
                                     res[0][:]).then_inc(agg_clear.sem, 16)

                    def store(s):
                        precompute(sp, val_sb.after(2 * s.g + 2), fmax_sb.after(s.g + 1), logit_sb.after(s.g + 1))
                        sp.wait_ge(ready.sem, 1)
                        sp.wait_ge(val_sb.sem, val_sb.after(2 * s.g + 2))
                        sp.wait_ge(fmax_sb.sem, fmax_sb.after(s.g + 1))
                        sp.wait_ge(logit_sb.sem, logit_sb.after(s.g + 1))
                        sp.dma_start(values_dram[bass.ds(s.g * CHUNK, CHUNK), :].rearrange("(t p) c -> p t c", p=P),
                                     gate_v[s.slot][:]).then_inc(values_out[s.slot].sem, 16)
                        for table, what in ((logit_dram, lg), (fmax_dram, fm)):
                            sp.dma_start(table[:, bass.ds(s.g * CHUNK, CHUNK)], what[s.slot][:]) \
                                .then_inc(values_out[s.slot].sem, 16)

                    pipeline(sp, chunks, [(load_scalars, 0), (load_vectors, 1), (load_indices, 2), (clear, 2),
                                          (load_penalties, 4), (store, 6)])
                    for k in range(2):
                        sp.wait_ge(values_out[k].sem, values_out[k].after(chunks // 2))
                    sp.wait_ge(agg_clear.sem, agg_clear.after(chunks))

                @block.gpsimd
                def _(pool):
                    def gather(s):
                        precompute(pool, idx_in[s.slot].after(s.half + 1), mid_step.after((s.g - 1) * steps))
                        pool.wait_ge(ready.sem, 1)
                        pool.wait_ge(idx_in[s.slot].sem, idx_in[s.slot].after(s.half + 1))
                        pool.wait_ge(mid_step.sem, mid_step.after((s.g - 1) * steps))
                        for table, to, first, sig in ((src_table, work, 0, rows_in), (dst_table, y, TILES, rows_b_in)):
                            for t in range(TILES):
                                pool.indirect_dma_start(
                                    to[s.slot][:, t, :], None, table,
                                    bass.IndirectOffsetOnAxis(idx[s.slot][:, first + t:first + t + 1], 0),
                                ).then_inc(sig[s.slot].sem, 16)

                    def root1(s):
                        st = stats[s.slot]
                        precompute(pool, var1_step.after((s.g + 1) * 2))
                        pool.wait_ge(ready.sem, 1)
                        pool.wait_ge(var1_step.sem, var1_step.after((s.g + 1) * 2))
                        pool.tensor_tensor(st[:, 36:40], st[:, 32:36], power[:, 0:TILES], ALU.pow).then_inc(root_sb.sem, 1)

                    def root2(s):
                        st = stats[s.slot]
                        precompute(pool, var2_step.after((s.g + 1) * 5))
                        pool.wait_ge(ready.sem, 1)
                        pool.wait_ge(var2_step.sem, var2_step.after((s.g + 1) * 5))
                        pool.tensor_tensor(st[:, 56:64], st[:, 48:56], power[:], ALU.pow).then_inc(root2_sb.sem, 1)

                    pipeline(pool, chunks, [(root1, 0), (root2, 2), (gather, 3)])

                @block.tensor
                def _(pe):
                    def hidden(s, lhs, weights, to, sig):
                        for t in range(TILES):
                            last = pe.matmul(psum[:, to, 64 * t:64 * t + 64], lhs[:, t * P:(t + 1) * P], W(weights),
                                             start=True, stop=True)
                        last.then_inc(sig.sem, 1)

                    def h1(s):
                        precompute(pe, hid_in[s.slot].after(s.half + 1), sq1_sb.after(s.g))
                        pe.wait_ge(ready.sem, 1)
                        pe.wait_ge(hid_in[s.slot].sem, hid_in[s.slot].after(s.half + 1))
                        pe.wait_ge(sq1_sb.sem, sq1_sb.after(s.g))
                        hidden(s, scal_t[s.slot], "rw1", 4, h1_mm)

                    def h2(s):
                        precompute(pe, h1t_sb.after(s.g + 1), sq2_sb.after(s.g))
                        pe.wait_ge(ready.sem, 1)
                        pe.wait_ge(h1t_sb.sem, h1t_sb.after(s.g + 1))
                        pe.wait_ge(sq2_sb.sem, sq2_sb.after(s.g))
                        hidden(s, hid_t, "rw2", 5, h2_mm)

                    def transposed(of, sig):
                        for t in range(TILES):
                            last = pe.transpose(psum[0:64, 6, t * P:(t + 1) * P], of[:, t, :], ident)
                        last.then_inc(sig.sem, 1)

                    def t1(s):
                        precompute(pe, silu1_sb.after(s.g + 1), h2t_sb.after(s.g - 2))
                        pe.wait_ge(ready.sem, 1)
                        pe.wait_ge(silu1_sb.sem, silu1_sb.after(s.g + 1))
                        pe.wait_ge(h2t_sb.sem, h2t_sb.after(s.g - 2))
                        transposed(hu[s.slot], h1t_mm)

                    def t2(s):
                        precompute(pe, silu2_sb.after(s.g + 1), h1t_sb.after(ahead(s.g, 3, chunks)))
                        pe.wait_ge(ready.sem, 1)
                        pe.wait_ge(silu2_sb.sem, silu2_sb.after(s.g + 1))
                        pe.wait_ge(h1t_sb.sem, h1t_sb.after(ahead(s.g, 3, chunks)))
                        transposed(hu_b[s.slot], h2t_mm)

                    def weights(s):
                        pe.wait_ge(h2t_sb.sem, h2t_sb.after(s.g + 1))
                        for r in range(2):
                            pe.wait_ge(w_sb.sem, w_sb.after(2 * s.g + r))
                            for t in range(2):
                                cut = slice((2 * r + t) * P, (2 * r + t + 1) * P)
                                last = pe.matmul(psum[:, 7, 224 * t:224 * t + 224], hid2_t[:, cut], W("rw3"),
                                                 start=True, stop=True)
                            last.then_inc(w_mm.sem, 1)

                    def messages_t(s):
                        pe.wait_ge(mid_step.sem, mid_step.after((s.g + 1) * steps))
                        for k in range(4):
                            pe.wait_ge(agg_sb.sem, agg_sb.after(4 * s.g + k - 1))
                            n = 97 if k == 0 else P
                            at = 0 if k == 0 else 97 + P * (k - 1)
                            for t in range(TILES):
                                last = pe.transpose(psum[0:n, k % 2, t * P:(t + 1) * P], mid[s.slot][:, t, at:at + n], ident)
                            last.then_inc(agg_mm.sem, 1)

                    def alpha(s):
                        precompute(pe, agg_sb.after(4 * s.g + 1), logit_sb.after(s.g))
                        pe.wait_ge(ready.sem, 1)
                        pe.wait_ge(agg_sb.sem, agg_sb.after(4 * s.g + 1))
                        pe.wait_ge(logit_sb.sem, logit_sb.after(s.g))
                        pe.matmul(bank(2, 64), W("lin_s", cols=(0, 64)), mid_t[0:97, 0, :], start=True, stop=True) \
                            .then_inc(alpha_mm.sem, 1)

                    def values(s):
                        pe.wait_ge(agg_sb.sem, agg_sb.after(4 * s.g + 4))
                        for r in range(2):
                            pe.wait_ge(val_sb.sem, val_sb.after(2 * s.g + r))
                            for t in range(2):
                                cut = slice((2 * r + t) * P, (2 * r + t + 1) * P)
                                pe.matmul(psum[:, 3, D * t:D * t + 64], mid_t[0:97, 0, cut], W("lin_s", cols=(64, 128)),
                                          start=True, stop=True)
                                for i in range(3):
                                    last = pe.matmul(psum[:, 3, D * t + 64 + 32 * i:D * t + 96 + 32 * i],
                                                     mid_t[:, 1 + i, cut], W("lin_v"), start=True, stop=True)
                            last.then_inc(val_mm.sem, 1)

                    def logits(s):
                        precompute(pe, leaky_step.after((s.g + 1) * 2))
                        pe.wait_ge(ready.sem, 1)
                        pe.wait_ge(leaky_step.sem, leaky_step.after((s.g + 1) * 2))
                        pe.matmul(bank(2, HEADS), W("adot"), leaky_t[:, :], start=True, stop=True) \
                            .then_inc(logit_mm.sem, 1)

                    pipeline(pe, chunks, [(h1, 0), (h2, 2), (messages_t, 5), (alpha, 5), (t1, 1), (t2, 3),
                                          (values, 5), (weights, 3), (logits, 5)])

                @block.scalar
                def _(act):
                    def squares(s, to, h, at, mm, sig, used, n, norm, m):
                        act.wait_ge(mm.sem, mm.after(s.g + 1))
                        act.wait_ge(used.sem, used.after((s.g - 1) * n))
                        act.wait_ge(norm.sem, norm.after((s.g - 1) * m))
                        ps = psum[:, at, 0:256].rearrange("p (t c) -> p t c", t=TILES)
                        act.activation(h[s.slot][:], ps, ACT.Copy)
                        act.activation(to[s.slot][:], ps, ACT.Square).then_inc(sig.sem, 1)

                    def tanh(s, to, of, done, n, sig):
                        act.wait_ge(done.sem, done.after((s.g + 1) * n))
                        act.activation(to[s.slot][:], of[s.slot][:], ACT.Tanh, scale=0.5).then_inc(sig.sem, 1)

                    def copy_t(s, to, mm, used, n, sig):
                        act.wait_ge(mm.sem, mm.after(s.g + 1))
                        act.wait_ge(used.sem, used.after(n))
                        act.activation(to[0:64, :], bank(6, 64), ACT.Copy).then_inc(sig.sem, 1)

                    def messages_t(s):
                        act.wait_ge(val_mm.sem, val_mm.after(2 * s.g))
                        act.wait_ge(alpha_mm.sem, alpha_mm.after(s.g))
                        for k in range(4):
                            n = 97 if k == 0 else P
                            act.wait_ge(agg_mm.sem, agg_mm.after(4 * s.g + k + 1))
                            act.activation(mid_t[0:n, k, :], bank(k % 2, n), ACT.Copy).then_inc(agg_sb.sem, 1)

                    def alpha(s):
                        act.wait_ge(alpha_mm.sem, alpha_mm.after(s.g + 1))
                        act.wait_ge(leaky_step.sem, leaky_step.after(s.g * 2))
                        act.activation(alpha_t[:, :], bank(2, 64), ACT.Tanh, scale=0.5).then_inc(alpha_sb.sem, 1)

                    def values(s):
                        act.wait_ge(values_out[s.slot].sem, values_out[s.slot].after(s.half))
                        for r in range(2):
                            act.wait_ge(val_mm.sem, val_mm.after(2 * s.g + r + 1))
                            ps = psum[:, 3, 0:2 * D].rearrange("p (t c) -> p t c", t=2)
                            to = gate_v[s.slot][:, 2 * r:2 * r + 2]
                            act.activation(to[:, :, 0:64], ps[:, :, 0:64], ACT.Copy)
                            act.activation(to[:, :, 64:].rearrange("p t (c i) -> p t i c", i=3),
                                           ps[:, :, 64:].rearrange("p t (i c) -> p t i c", i=3), ACT.Copy) \
                                .then_inc(val_sb.sem, 1)

                    def weights(s):
                        act.wait_ge(mid_step.sem, mid_step.after((s.g - 1) * steps))
                        for r in range(2):
                            act.wait_ge(w_mm.sem, w_mm.after(2 * s.g + r + 1))
                            act.activation(radial[s.slot][:, 2 * r:2 * r + 2, :],
                                           psum[:, 7, 0:448].rearrange("p (t c) -> p t c", t=2), ACT.Copy) \
                                .then_inc(w_sb.sem, 1)

                    def logits(s):
                        act.wait_ge(logit_mm.sem, logit_mm.after(s.g + 1))
                        act.activation(lg[s.slot][:], bank(2, HEADS), ACT.Copy).then_inc(logit_sb.sem, 1)

                    pipeline(act, chunks, [
                        (lambda s: squares(s, sq, h1_rows, 4, h1_mm, sq1_sb, var1_step, 2, ln1_step, 3), 0),
                        (lambda s: squares(s, sq_b, h2_rows, 5, h2_mm, sq2_sb, var2_step, 5, ln2_step, 4), 2),
                        (lambda s: tanh(s, hu, hn, ln1_step, 3, th1_sb), 1),
                        (messages_t, 5),
                        (lambda s: tanh(s, hu_b, hn_b, ln2_step, 4, th2_sb), 3),
                        (alpha, 5),
                        (lambda s: copy_t(s, hid_t, h1t_mm, h2_mm, s.g, h1t_sb), 1),
                        (lambda s: copy_t(s, hid2_t, h2t_mm, w_mm, 2 * s.g, h2t_sb), 3),
                        (values, 5), (weights, 3), (logits, 5)])

                @block.vector
                def _(dve):
                    def var1(s):
                        chain = Chain(var1_step, s.g, 2)
                        dve.wait_ge(chain.sem, chain.after(0))
                        st = stats[s.slot]
                        dve.wait_ge(sq1_sb.sem, sq1_sb.after(s.g + 1))
                        dve.wait_ge(root_sb.sem, root_sb.after(s.g - 1))
                        k = chain.did(dve.tensor_reduce(st[:, 28:32], sq[s.slot][:], AX_X, ALU.add).then_inc(chain.sem, 1))
                        dve.wait_ge(chain.sem, chain.after(k))
                        chain.did(dve.tensor_scalar(st[:, 32:36], st[:, 28:32], 1.0 / 64, 1e-5, ALU.mult, ALU.add).then_inc(chain.sem, 1))
                        chain.end()

                    def var2(s):
                        chain = Chain(var2_step, s.g, 5)
                        dve.wait_ge(chain.sem, chain.after(0))
                        st = stats[s.slot]
                        dve.wait_ge(sq2_sb.sem, sq2_sb.after(s.g + 1))
                        dve.wait_ge(attr_in[s.slot].sem, attr_in[s.slot].after(s.half + 1))
                        dve.wait_ge(root2_sb.sem, root2_sb.after(s.g - 1))
                        v = attr[s.quad][:, :, 1:4]
                        a = chain.did(dve.tensor_tensor(vec_sq[s.slot][:], v, v, ALU.mult).then_inc(chain.sem, 1))
                        b = chain.did(dve.tensor_reduce(st[:, 64:68], sq_b[s.slot][:], AX_X, ALU.add).then_inc(chain.sem, 1))
                        dve.wait_ge(chain.sem, chain.after(a))
                        a = chain.did(dve.tensor_reduce(st[:, 68:72], vec_sq[s.slot][:], AX_X, ALU.add).then_inc(chain.sem, 1))
                        dve.wait_ge(chain.sem, chain.after(b))
                        chain.did(dve.tensor_scalar(st[:, 48:52], st[:, 64:68], 1.0 / 64, 1e-5, ALU.mult, ALU.add).then_inc(chain.sem, 1))
                        dve.wait_ge(chain.sem, chain.after(a))
                        chain.did(dve.tensor_scalar(st[:, 52:56], st[:, 68:72], 1e-12, None, ALU.add).then_inc(chain.sem, 1))
                        chain.end()

                    def norm(s, chain, h, roots, to, g, b):
                        all_ = [P, TILES, 64]
                        k = chain.did(dve.tensor_tensor(
                            to[s.slot][:], h[s.slot][:],
                            spread(roots, 2, all_), ALU.mult).then_inc(chain.sem, 1))
                        dve.wait_ge(chain.sem, chain.after(k))
                        k = chain.did(dve.tensor_tensor(to[s.slot][:], to[s.slot][:], spread(W(g), 1, all_), ALU.mult).then_inc(chain.sem, 1))
                        dve.wait_ge(chain.sem, chain.after(k))
                        return chain.did(dve.tensor_tensor(to[s.slot][:], to[s.slot][:], spread(W(b), 1, all_), ALU.add).then_inc(chain.sem, 1))

                    def ln1(s):
                        chain = Chain(ln1_step, s.g, 3)
                        dve.wait_ge(chain.sem, chain.after(0))
                        dve.wait_ge(root_sb.sem, root_sb.after(s.g + 1))
                        dve.wait_ge(silu1_sb.sem, silu1_sb.after(s.g - 1))
                        norm(s, chain, h1_rows, stats[s.slot][:, 36:40], hn, "rg1", "rbe1")
                        chain.end()

                    def ln2(s):
                        chain = Chain(ln2_step, s.g, 4)
                        dve.wait_ge(chain.sem, chain.after(0))
                        dve.wait_ge(root2_sb.sem, root2_sb.after(s.g + 1))
                        dve.wait_ge(silu2_sb.sem, silu2_sb.after(s.g - 1))
                        chain.did(dve.tensor_tensor(
                            attr[s.quad][:, :, 1:6], attr[s.quad][:, :, 1:6],
                            spread(stats[s.slot][:, 60:64], 2, [P, TILES, 5]), ALU.mult).then_inc(chain.sem, 1))
                        norm(s, chain, h2_rows, stats[s.slot][:, 56:60], hn_b, "rg2", "rbe2")
                        chain.end()

                    def silu(s, h, th, done, sig, used):
                        dve.wait_ge(done.sem, done.after(s.g + 1))
                        dve.wait_ge(used.sem, used.after(s.g - 1))
                        dve.scalar_tensor_tensor(th[s.slot][:], th[s.slot][:], 1.0, h[s.slot][:], ALU.add, ALU.mult) \
                            .then_inc(sig.sem, 1)

                    def message(s):
                        chain = Chain(mid_step, s.g, steps)
                        dve.wait_ge(chain.sem, chain.after(0))
                        dve.wait_ge(rows_in[s.slot].sem, rows_in[s.slot].after(s.half + 1))
                        dve.wait_ge(rows_b_in[s.slot].sem, rows_b_in[s.slot].after(s.half + 1))
                        dve.wait_ge(w_sb.sem, w_sb.after(2 * s.g + 2))
                        dve.wait_ge(agg_mm.sem, agg_mm.after(4 * (s.g - 1)))
                        e = e_ext[s.slot]
                        chain.did(dve.tensor_tensor(e[:, :, 0:D], work[s.slot][:], y[s.slot][:], ALU.add).then_inc(chain.sem, 1))
                        k = chain.did(dve.tensor_tensor(e[:, :, D:], work[s.slot][:, :, C0:C0 + 64],
                                                        y[s.slot][:, :, C0:C0 + 64], ALU.add).then_inc(chain.sem, 1))
                        dve.wait_ge(ln2_step.sem, ln2_step.after((s.g + 1) * 4))
                        dve.wait_ge(chain.sem, chain.after(k))
                        messages(dve, s.slot, chain, e, radial[s.slot], attr[s.quad], False, True)
                        chain.end()

                    def leaky(s):
                        chain = Chain(leaky_step, s.g, 2)
                        dve.wait_ge(chain.sem, chain.after(0))
                        dve.wait_ge(alpha_sb.sem, alpha_sb.after(s.g + 1))
                        dve.wait_ge(logit_mm.sem, logit_mm.after(s.g))
                        k = chain.did(dve.tensor_scalar(leaky_t[:, :], alpha_t[:, :], 0.4, 0.6, ALU.mult, ALU.add).then_inc(chain.sem, 1))
                        dve.wait_ge(chain.sem, chain.after(k))
                        chain.did(dve.tensor_tensor(leaky_t[:, :], leaky_t[:, :], bank(2, 64), ALU.mult).then_inc(chain.sem, 1))
                        chain.end()

                    def running_max(s):
                        dve.wait_ge(logit_sb.sem, logit_sb.after(s.g + 1))
                        dve.wait_ge(fmax_sb.sem, fmax_sb.after(s.g))
                        dve.wait_ge(pre_in[s.slot].sem, pre_in[s.slot].after(s.half + 1))
                        dve.wait_ge(values_out[s.slot].sem, values_out[s.slot].after(s.half))
                        dve.tensor_tensor_scan(fm[s.slot][:], pen[s.slot][:], lg[s.slot][:],
                                               fm[1 - s.slot][:, CHUNK - 1:CHUNK], ALU.add, ALU.max) \
                            .then_inc(fmax_sb.sem, 1)

                    pipeline(dve, chunks, [
                        (ln1, 1), (var1, 0), (ln2, 3),
                        (lambda s: silu(s, hn, hu, th1_sb, silu1_sb, h1t_mm), 1), (var2, 2),
                        (lambda s: silu(s, hn_b, hu_b, th2_sb, silu2_sb, h2t_mm), 3),
                        (leaky, 5), (message, 4), (running_max, 5)])
            for sig in (h1_mm, h2_mm, h1t_mm, h2t_mm, sq1_sb, sq2_sb, th1_sb, th2_sb, h1t_sb, h2t_sb,
                        silu1_sb, silu2_sb, alpha_mm, alpha_sb, logit_mm, logit_sb, fmax_sb,
                        root_sb, root2_sb, agg_clear):
                sig.passed(chunks)
            for sig, n in ((w_mm, 2), (w_sb, 2), (val_mm, 2), (val_sb, 2), (agg_mm, 4), (agg_sb, 4),
                           (mid_step, steps), (var1_step, 2), (var2_step, 5), (ln1_step, 3), (ln2_step, 4),
                           (leaky_step, 2)):
                sig.passed(n * chunks)
            for sig in (*idx_in, *hid_in, *attr_in, *pre_in, *rows_in, *rows_b_in, *values_out):
                sig.passed(chunks // 2)

        def edge_softmax():
            with ExitStack() as own, nc.Block() as block:
                pen, lg, ex, bx = (two(n, [HEADS, CHUNK], own=own)
                                   for n in ("pen_back", "logits", "differences", "exponentials"))

                @block.sync
                def _(sp):
                    def load(s):
                        c = chunks - 1 - s.g
                        precompute(sp, pre_step.after((s.g - 1) * 3))
                        sp.wait_ge(ready.sem, 1)
                        sp.wait_ge(pre_step.sem, pre_step.after((s.g - 1) * 3))
                        sp.dma_start(idx[s.slot][:], inp["edge_idx"][bass.ds(c, 1)].rearrange("o p t -> (o p) t")) \
                            .then_inc(idx_in[s.slot].sem, 16)
                        load_dst_row(sp, s.slot, c).then_inc(edge_in[s.slot].sem, 16)
                        sp.dma_start(lg[s.slot][:], logit_dram[:, bass.ds(c * CHUNK, CHUNK)]) \
                            .then_inc(edge_in[s.slot].sem, 16)
                        sp.dma_start(fm[s.slot][:], fmax_dram[:, bass.ds(c * CHUNK, CHUNK)]) \
                            .then_inc(edge_in[s.slot].sem, 16)
                        sp.dma_start(pen[s.slot][:], pen_dram[0, bass.ds(c * CHUNK + 1, CHUNK)].partition_broadcast(HEADS)) \
                            .then_inc(vec_in[s.slot].sem, 16)
                        precompute(sp, mid_step.after((s.g - 1) * 2))
                        sp.wait_ge(ready.sem, 1)
                        sp.wait_ge(mid_step.sem, mid_step.after((s.g - 1) * 2))
                        sp.dma_start(gate_v[s.slot][:], values_dram[bass.ds(c * CHUNK, CHUNK), :]
                                     .rearrange("(t p) c -> p t c", p=P)).then_inc(vec_in[s.slot].sem, 16)

                    pipeline(sp, chunks, [
                        (load, 0), (lambda s: load_sidx(sp, s, chunks - 1 - s.g), 1),
                        (lambda s: store_ends(sp, s, chunks - 1 - s.g), 2)])
                    for k in range(2):
                        sp.wait_ge(ends_out[k].sem, ends_out[k].after(chunks // 2))

                @block.gpsimd
                def _(pool):
                    pipeline(pool, chunks, [(lambda s: scatter(pool, s), 0)])
                    for k in range(2):
                        pool.wait_ge(scattered[k].sem, scattered[k].after(chunks // 2))

                @block.vector
                def _(dve):
                    def maxima(s):
                        chain = Chain(pre_step, s.g, 3)
                        dve.wait_ge(chain.sem, chain.after(0))
                        dve.wait_ge(edge_in[s.slot].sem, edge_in[s.slot].after(s.half + 1))
                        dve.wait_ge(vec_in[s.slot].sem, vec_in[s.slot].after(s.half + 1))
                        dve.wait_ge(idx_in[s.slot].sem, idx_in[s.slot].after(s.half + 1))
                        dve.wait_ge(sc_mm.sem, sc_mm.after(s.g - 1))
                        k = chain.did(dve.tensor_tensor_scan(
                            bm[s.slot][:, ::-1], pen[s.slot][:, ::-1], fm[s.slot][:, ::-1],
                            bm[1 - s.slot][:, 0:1], ALU.add, ALU.max).then_inc(chain.sem, 1))
                        segment_matrix(dve, s.slot, chain)
                        dve.wait_ge(chain.sem, chain.after(k))
                        dve.wait_ge(gate_sb.sem, gate_sb.after(s.g - 1))
                        chain.did(dve.tensor_tensor(ex[s.slot][:], lg[s.slot][:], bm[s.slot][:], ALU.subtract).then_inc(chain.sem, 1))
                        chain.end()

                    def weigh(s):
                        chain = Chain(mid_step, s.g, 2)
                        dve.wait_ge(chain.sem, chain.after(0))
                        dve.wait_ge(xt_sb.sem, xt_sb.after(s.g + 1))
                        dve.wait_ge(sc_mm.sem, sc_mm.after(s.g - 1))
                        m, v = aux[s.slot], gate_v[s.slot]
                        for at, n in ((0, 8), (64, 12)):
                            chain.did(dve.tensor_tensor(
                                m[:, :, at:at + HEADS * n].rearrange("p t (h k) -> p t h k", h=HEADS),
                                v[:, :, at:at + HEADS * n].rearrange("p t (h k) -> p t h k", h=HEADS),
                                spread(m[:, :, D:D + HEADS], 3, [P, TILES, HEADS, n]), ALU.mult).then_inc(chain.sem, 1))
                        chain.end()

                    pipeline(dve, chunks, [(maxima, 0), (weigh, 1)])

                @block.scalar
                def _(act):
                    def exponentials(s):
                        act.wait_ge(pre_step.sem, pre_step.after((s.g + 1) * 3))
                        act.wait_ge(xt_mm.sem, xt_mm.after(s.g - 1))
                        act.activation(bx[s.slot][:], ex[s.slot][:], ACT.Exp).then_inc(gate_sb.sem, 1)

                    def copy(s):
                        act.wait_ge(xt_mm.sem, xt_mm.after(s.g + 1))
                        act.wait_ge(sc_mm.sem, sc_mm.after(s.g - 1))
                        act.activation(aux[s.slot][:, :, D:D + HEADS],
                                       psum[:, s.slot, 0:32].rearrange("p (t h) -> p t h", t=TILES), ACT.Copy) \
                            .then_inc(xt_sb.sem, 1)

                    def sums(s):
                        act.wait_ge(sc_mm.sem, sc_mm.after(s.g + 1))
                        act.wait_ge(scattered[s.slot].sem, scattered[s.slot].after(s.half))
                        act.wait_ge(ends_out[s.slot].sem, ends_out[s.slot].after(s.half))
                        act.activation(res[s.slot][:, :, 0:D + HEADS], tiled(2 + 2 * s.slot, D + HEADS), ACT.Copy) \
                            .then_inc(res_sb.sem, 1)

                    pipeline(act, chunks, [(exponentials, 0), (copy, 0), (sums, 1)])

                @block.tensor
                def _(pe):
                    def turn(s):
                        precompute(pe, gate_sb.after(s.g + 1), xt_sb.after(s.g - 1))
                        pe.wait_ge(ready.sem, 1)
                        pe.wait_ge(gate_sb.sem, gate_sb.after(s.g + 1))
                        pe.wait_ge(xt_sb.sem, xt_sb.after(s.g - 1))
                        for t in range(TILES):
                            last = pe.transpose(psum[:, s.slot, 8 * t:8 * t + 8], bx[s.slot][:, t * P:(t + 1) * P],
                                                W("ident", (0, HEADS), (0, HEADS)))
                        last.then_inc(xt_mm.sem, 1)

                    def sums(s):
                        pe.wait_ge(mid_step.sem, mid_step.after((s.g + 1) * 2))
                        pe.wait_ge(res_sb.sem, res_sb.after(s.g - 1))
                        for t in range(TILES):
                            last = pe.matmul(tiled(2 + 2 * s.slot, D + HEADS)[:, t], seg[s.slot][:, t, :],
                                             aux[s.slot][:, t, 0:D + HEADS], start=True, stop=True)
                        last.then_inc(sc_mm.sem, 1)

                    pipeline(pe, chunks, [(turn, 0), (sums, 1)])
            for sig in (xt_mm, xt_sb, sc_mm, gate_sb, res_sb):
                sig.passed(chunks)
            pre_step.passed(3 * chunks)
            mid_step.passed(2 * chunks)
            for sig in (*idx_in, *edge_in, *vec_in, *sidx_in, *scattered, *ends_out):
                sig.passed(chunks // 2)

        def node_first():
            den_steps, x1_steps, scale_steps, hidden_steps = 4, 2 * TILES + 5, 2 + 2 * TILES, 3
            sum_steps = 2 * TILES + 1 + 2 * TILES + 2
            m_at, q_at, v_at, r_at, c_at = 48, 56, 64, 72, 80
            with ExitStack() as own, nc.Block() as block:
                scaled = two("scaled", [P, TILES, ROW], own=own)
                ht = [sb(f"ht_{k}", [P, CHUNK], own=own) for k in range(5)]
                xs2_t, xv2_t = sb("xs2_t", [65, CHUNK], own=own), sb("xv2_t", [96, CHUNK], own=own)

                @block.sync
                def _(sp):
                    pipeline(sp, chunks, [
                        (lambda s: load_nodes(sp, s, x_rows[0], sum_step, sum_steps, den_steps), 0),
                        (lambda s: store_nodes(sp, s, x_rows[1]), 5)])
                    for k in range(2):
                        sp.wait_ge(node_out[k].sem, node_out[k].after(chunks // 2))

                @block.tensor
                def _(pe):
                    def turn_sums(s):
                        precompute(pe, pre_step.after((s.g + 1) * den_steps), xt2_sb.after(s.g - 1), xt_sb.after(s.g))
                        pe.wait_ge(ready.sem, 1)
                        pe.wait_ge(pre_step.sem, pre_step.after((s.g + 1) * den_steps))
                        pe.wait_ge(xt2_sb.sem, xt2_sb.after(s.g - 1))
                        pe.wait_ge(xt_sb.sem, xt_sb.after(s.g))
                        transpose_rows(pe, aux[s.slot], C0, C0, 0).then_inc(xt_mm.sem, 1)

                    def turn_norm(s):
                        precompute(pe, scale_step.after((s.g + 1) * scale_steps), xt_sb.after(ahead(s.g, 2, chunks)))
                        pe.wait_ge(ready.sem, 1)
                        pe.wait_ge(scale_step.sem, scale_step.after((s.g + 1) * scale_steps))
                        pe.wait_ge(xt_sb.sem, xt_sb.after(ahead(s.g, 2, chunks)))
                        transpose_rows(pe, scaled[s.slot], C0 + 1, C0 + 1, 0).then_inc(xt2_mm.sem, 1)

                    def project(s):
                        pe.wait_ge(xt_sb.sem, xt_sb.after(s.g + 1))
                        pe.wait_ge(sum_step.sem, sum_step.after((s.g - 1) * sum_steps))
                        pe.wait_ge(mid_step.sem, mid_step.after(s.g * x1_steps))
                        to = tiled(2, D)
                        for t in range(TILES):
                            cut = slice(t * P, (t + 1) * P)
                            pe.matmul(to[:, t, 0:C0], xs_t[:, cut], W("proj_s"), start=True, stop=True)
                            last = pe.matmul(to[:, t, C0:], xv_t[:, cut], W("proj_v"), start=True, stop=True)
                        last.then_inc(sc_mm.sem, 1)

                    def hidden(s):
                        pe.wait_ge(xt2_sb.sem, xt2_sb.after(s.g + 1))
                        pe.wait_ge(hidden_step.sem, hidden_step.after(s.g * hidden_steps))
                        pe.matmul(bank(4), W("f1_s"), xs2_t[:, :], start=True, stop=True)
                        pe.matmul(bank(5), W("f1_g"), xs2_t[:, :], start=True, stop=True)
                        pe.matmul(bank(6), W("f1_v", cols=(0, 128)), xv2_t[:, :], start=True, stop=True)
                        pe.matmul(bank(7, 64), W("f1_v", cols=(128, 192)), xv2_t[:, :], start=True, stop=True) \
                            .then_inc(hidden_mm.sem, 1)

                    def outputs(s):
                        pe.wait_ge(hidden_step.sem, hidden_step.after((s.g + 1) * hidden_steps))
                        pe.wait_ge(mid_step.sem, mid_step.after(ahead(s.g, 2, chunks) * x1_steps))
                        to = tiled(2, D)
                        for t in range(TILES):
                            cut = slice(t * P, (t + 1) * P)
                            pe.matmul(to[:, t, 0:C0], W("ones", (0, 1), (0, P)), W("f2_b"), start=True, stop=False)
                            pe.matmul(to[:, t, 0:C0], ht[2][:, cut], W("f2_s"), start=False, stop=True)
                            pe.matmul(to[:, t, C0:C0 + 64], ht[3][:, cut], W("f2_v"), start=True, stop=True)
                            last = pe.matmul(to[:, t, C0 + 64:], ht[4][0:64, cut], W("f2_v", (0, 64), (0, 32)),
                                             start=True, stop=True)
                        last.then_inc(post_mm.sem, 1)

                    pipeline(pe, chunks, [(turn_norm, 2), (hidden, 2), (project, 1), (turn_sums, 0), (outputs, 2)])

                @block.scalar
                def _(act):
                    def copy(s, to_s, to_v, rows_s, mm, used, sig):
                        act.wait_ge(mm.sem, mm.after(s.g + 1))
                        act.wait_ge(used.sem, used.after(s.g))
                        act.activation(to_s[0:rows_s, :], bank(0, rows_s), ACT.Copy)
                        act.activation(to_v[:, :], bank(1, 96), ACT.Copy).then_inc(sig.sem, 1)

                    def gates(s):
                        act.wait_ge(hidden_mm.sem, hidden_mm.after(s.g + 1))
                        act.wait_ge(hidden_step.sem, hidden_step.after(s.g * hidden_steps))
                        act.activation(ht[0][:, :], bank(4), ACT.Tanh, scale=0.5)
                        act.activation(ht[1][:, :], bank(5), ACT.Tanh, scale=0.5).then_inc(gate_sb.sem, 1)

                    pipeline(act, chunks, [
                        (lambda s: copy(s, xs2_t, xv2_t, C0 + 1, xt2_mm, hidden_mm, xt2_sb), 2),
                        (gates, 2),
                        (lambda s: copy(s, xs_t, xv_t, C0, xt_mm, sc_mm, xt_sb), 0),
                        (lambda s: final_norm(act, s), 4)])

                @block.gpsimd
                def _(pool):
                    pipeline(pool, chunks, [
                        (lambda s: root(pool, s, 32, TILES, sum_step, sum_steps, root2_sb), 3),
                        (lambda s: root(pool, s, v_at, 2 * TILES, mid_step, x1_steps, root_sb), 1)])

                @block.vector
                def _(dve):
                    def divide(s):
                        chain = Chain(pre_step, s.g, den_steps)
                        dve.wait_ge(chain.sem, chain.after(0))
                        sums, to = agg[s.quad], aux[s.slot]
                        dve.wait_ge(node_in[s.slot].sem, node_in[s.slot].after(s.half + 1))
                        dve.wait_ge(mid_step.sem, mid_step.after((s.g - 1) * x1_steps))
                        dve.wait_ge(xt_mm.sem, xt_mm.after(s.g - 1))
                        r = to[:, :, D:D + HEADS]
                        k = chain.did(dve.tensor_scalar(r, sums[:, :, D:D + HEADS], 1e-12, None, ALU.add).then_inc(chain.sem, 1))
                        dve.wait_ge(chain.sem, chain.after(k))
                        k = chain.did(dve.reciprocal(r, r).then_inc(chain.sem, 1))
                        dve.wait_ge(chain.sem, chain.after(k))
                        for at, n in ((0, 8), (C0, 12)):
                            chain.did(dve.tensor_tensor(
                                to[:, :, at:at + HEADS * n].rearrange("p t (h k) -> p t h k", h=HEADS),
                                sums[:, :, at:at + HEADS * n].rearrange("p t (h k) -> p t h k", h=HEADS),
                                spread(r, 3, [P, TILES, HEADS, n]), ALU.mult).then_inc(chain.sem, 1))
                        chain.end()

                    def residual(s):
                        chain = Chain(mid_step, s.g, x1_steps)
                        dve.wait_ge(chain.sem, chain.after(0))
                        st, x1, sq_v = stats[s.slot], work[s.quad], aux[s.slot][:, :, 0:96]
                        dve.wait_ge(sc_mm.sem, sc_mm.after(s.g + 1))
                        dve.wait_ge(sum_step.sem, sum_step.after((s.g - 1) * sum_steps))
                        dve.wait_ge(scale_step.sem, scale_step.after((s.g - 1) * scale_steps))
                        dve.wait_ge(pre_step.sem, pre_step.after((s.g + 1) * den_steps))
                        dve.wait_ge(root_sb.sem, root_sb.after(s.g - 1))
                        k = chain.did(dve.tensor_tensor(x1[:], tiled(2, D), rows[s.quad][:, :, 0:D], ALU.add).then_inc(chain.sem, 1))
                        dve.wait_ge(chain.sem, chain.after(k))
                        a = chain.did(dve.tensor_tensor(sq_v, x1[:, :, C0:], x1[:, :, C0:], ALU.mult).then_inc(chain.sem, 1))
                        b = mean_var(dve, chain, st, x1[:, :, 0:C0], m_at)
                        dve.wait_ge(chain.sem, chain.after(max(a, b)))
                        k = chain.did(dve.tensor_reduce(st[:, q_at:q_at + 4], sq_v, AX_X, ALU.add).then_inc(chain.sem, 1))
                        chain.did(dve.tensor_scalar(st[:, v_at:v_at + 4], pairs(st, m_at, 1), 1e-5, None, ALU.add).then_inc(chain.sem, 1))
                        dve.wait_ge(chain.sem, chain.after(k))
                        chain.did(dve.tensor_scalar(st[:, v_at + 4:v_at + 8], st[:, q_at:q_at + 4], 1.0 / 96, 1e-5,
                                                    ALU.mult, ALU.add).then_inc(chain.sem, 1))
                        chain.end()

                    def scale(s):
                        chain = Chain(scale_step, s.g, scale_steps)
                        dve.wait_ge(chain.sem, chain.after(0))
                        st, x1, to, attrs = stats[s.slot], work[s.quad], scaled[s.slot], rows[s.quad][:, :, D:ROW]
                        dve.wait_ge(root_sb.sem, root_sb.after(s.g + 1))
                        dve.wait_ge(xt2_mm.sem, xt2_mm.after(s.g - 1))
                        a = chain.did(dve.tensor_tensor(
                            st[:, c_at:c_at + 8].rearrange("p (k t) -> p k t", k=2),
                            st[:, r_at:r_at + 8].rearrange("p (k t) -> p k t", k=2),
                            spread(rows[s.quad][:, :, D], 1, [P, 2, TILES]), ALU.mult).then_inc(chain.sem, 1))
                        chain.did(dve.tensor_copy(to[:, :, C0:C0 + 1], attrs).then_inc(chain.sem, 1))
                        dve.wait_ge(chain.sem, chain.after(a))
                        for t in range(TILES):
                            chain.did(dve.tensor_scalar(
                                to[:, t, 0:C0], x1[:, t, 0:C0], st[:, m_at + 2 * t:m_at + 2 * t + 1],
                                st[:, c_at + t:c_at + t + 1], ALU.subtract, ALU.mult).then_inc(chain.sem, 1))
                            chain.did(dve.tensor_scalar(
                                to[:, t, C0 + 1:], x1[:, t, C0:], st[:, c_at + 4 + t:c_at + 5 + t], None, ALU.mult).then_inc(chain.sem, 1))
                        chain.end()

                    def activate(s):
                        chain = Chain(hidden_step, s.g, hidden_steps)
                        dve.wait_ge(chain.sem, chain.after(0))
                        dve.wait_ge(gate_sb.sem, gate_sb.after(s.g + 1))
                        dve.wait_ge(post_mm.sem, post_mm.after(s.g))
                        for th, at, to, n in ((0, 4, 2, P), (1, 6, 3, P), (1, 7, 4, 64)):
                            chain.did(dve.scalar_tensor_tensor(ht[to][0:n, :], ht[th][0:n, :], 1.0, bank(at, n),
                                                               ALU.add, ALU.mult).then_inc(chain.sem, 1))
                        chain.end()

                    def combine(s):
                        chain = Chain(sum_step, s.g, sum_steps)
                        dve.wait_ge(chain.sem, chain.after(0))
                        x, x1, yy, out_ = rows[s.quad], work[s.quad], y[s.slot], tiled(2, D)
                        dve.wait_ge(post_mm.sem, post_mm.after(s.g + 1))
                        dve.wait_ge(norm_sb.sem, norm_sb.after(s.g - 1))
                        k = chain.did(dve.tensor_tensor(x1[:], x1[:], x[:, :, 0:D], ALU.add).then_inc(chain.sem, 1))
                        dve.wait_ge(chain.sem, chain.after(k))
                        for t in range(TILES):
                            def components(ap, order):
                                return ap[:, t, C0:D].rearrange(order, i=3)
                            chain.did(dve.scalar_tensor_tensor(
                                yy[:, t, 0:C0], out_[:, t, 0:C0], x[:, t, D:ROW], x1[:, t, 0:C0], ALU.mult, ALU.add).then_inc(chain.sem, 1))
                            k = chain.did(dve.scalar_tensor_tensor(
                                components(yy, "p (c i) -> p i c"), components(out_, "p (i c) -> p i c"),
                                x[:, t, D:ROW], components(x1, "p (c i) -> p i c"), ALU.mult, ALU.add).then_inc(chain.sem, 1))
                        dve.wait_ge(chain.sem, chain.after(k))
                        final_sums(dve, s, chain)
                        chain.end()

                    pipeline(dve, chunks, [(scale, 2), (combine, 3), (divide, 0), (residual, 1), (activate, 2),
                                           (lambda s: final_bias(dve, s), 4)])
            for sig in (xt_mm, xt_sb, xt2_mm, xt2_sb, sc_mm, hidden_mm, post_mm, gate_sb, root_sb, root2_sb,
                        bias_sb, norm_sb):
                sig.passed(chunks)
            for sig in (*node_in, *node_out):
                sig.passed(chunks // 2)
            for sig, n in ((pre_step, den_steps), (mid_step, x1_steps), (scale_step, scale_steps),
                           (hidden_step, hidden_steps), (sum_step, sum_steps)):
                sig.passed(n * chunks)

        def setup():
            pen_cols = tiles + 1
            folds = (("ln1_s", "sd_s"), ("ln2_s", "f1_s"), ("ln2_s", "f1_g"))
            loads, stores_after = 10, 4
            with ExitStack() as own, nc.Block() as block:
                def at_setup(name, shape, dt=F32):
                    return sb(name, shape, dt, own)

                cols, cols_next = at_setup("cols", [P, tiles], I32), at_setup("cols_next", [P, tiles], I32)
                prev, cur = at_setup("prev", [P, pen_cols], I32), at_setup("cur", [P, pen_cols], I32)
                same, scatter_to = at_setup("same", [P, tiles]), at_setup("scatter_to", [P, tiles], I32)
                drop = at_setup("drop", [P, pen_cols])
                first, first_next, last_prev, last = (
                    at_setup(n, [P, FIX_BLOCKS], I32) for n in ("first", "first_next", "last_prev", "last"))
                first_all = at_setup("first_all", [P, tiles], I32)
                ends_here, carried = at_setup("ends_here", [P, FIX_BLOCKS]), at_setup("carried", [P, FIX_BLOCKS])
                joined = at_setup("joined", [P, FIX_BLOCKS, tiles])
                mean = at_setup("mean", [P, 2])

                @block.gpsimd
                def _(pool):
                    parts = 2 * TILES
                    for k in range(parts):
                        r = slice(k * P // parts, (k + 1) * P // parts)
                        pool.dma_start(w_all[r], inp["weights"][r]).then_inc(scattered[k % 2].sem, 16)

                @block.sync
                def _(sp):
                    for to, of in (
                            (cols[:], inp["dst_cols"]), (cols_next[:], inp["dst_cols_next"]),
                            (prev[:], inp["dst_prev"]), (cur[:], inp["dst_cur"]),
                            (first[0:fix_rows], inp["tile_first"]), (first_next[0:fix_rows], inp["tile_first_next"]),
                            (last_prev[0:fix_rows], inp["tile_last_prev"]), (last[0:fix_rows], inp["tile_last"]),
                            (first_all[0:fix_rows], inp["tile_first_row"][0, 0:tiles].partition_broadcast(fix_rows)),
                            (join_mask[0:fix_rows], inp["triangle"])):
                        sp.dma_start(to, of).then_inc(setup_in.sem, 16)
                    sp.wait_ge(setup_step.sem, setup_step.after(stores_after))
                    sp.dma_start(sidx_dram.rearrange("c p t -> p c t"),
                                 scatter_to[:].rearrange("p (c t) -> p c t", t=TILES)).then_inc(setup_out.sem, 16)
                    sp.dma_start(pen_dram.rearrange("o (p m) -> (o p) m", m=pen_cols), drop[:]).then_inc(setup_out.sem, 16)
                    sp.wait_ge(setup_out.sem, setup_out.after(2))

                @block.tensor
                def _(pe):
                    for k in range(2):
                        pe.wait_ge(scattered[k].sem, scattered[k].after(1))
                    for k, (norm, weights) in enumerate(folds):
                        pe.matmul(bank(k, 65, 128), W(norm, cols=(0, 65)), W(weights), start=True, stop=True) \
                            .then_inc(setup_mm.sem, 1)

                @block.vector
                def _(dve):
                    for ap, value in ((half_pi[:], float(np.pi / 2)), (power[:], -0.5), (xs_t[64:65], 1.0),
                                      (hid_t[64:65], 1.0), (hid2_t[64:65], 1.0), (fm[1][:], 0.0), (bm[1][:], 0.0)):
                        dve.memset(ap, value)
                    for k in range(2):
                        dve.memset(mid[k][:, :, 96:97], 1.0)
                        dve.memset(res[k][:], 0.0)
                    chain = Chain(setup_step, 0, 0)
                    dve.wait_ge(chain.sem, chain.after(0))
                    dve.wait_ge(setup_in.sem, setup_in.after(loads))
                    k = chain.did(dve.tensor_tensor(same[:], cols[:], cols_next[:], ALU.is_equal).then_inc(chain.sem, 1))
                    dve.wait_ge(chain.sem, chain.after(k))
                    chain.did(dve.scalar_tensor_tensor(scatter_to[:], same[:], SKIP, cols[:], ALU.mult, ALU.add).then_inc(chain.sem, 1))
                    k = chain.did(dve.tensor_tensor(drop[:], prev[:], cur[:], ALU.subtract).then_inc(chain.sem, 1))
                    dve.wait_ge(chain.sem, chain.after(k))
                    assert chain.did(dve.tensor_scalar(drop[:], drop[:], NEG, None, ALU.mult).then_inc(chain.sem, 1)) == stores_after
                    r = slice(0, fix_rows)
                    k = chain.did(dve.tensor_tensor(
                        joined[r], spread(first_all[r], 1, [fix_rows, FIX_BLOCKS, tiles]),
                        spread(last[r], 2, [fix_rows, FIX_BLOCKS, tiles]), ALU.is_equal).then_inc(chain.sem, 1))
                    dve.wait_ge(chain.sem, chain.after(k))
                    chain.did(dve.tensor_tensor(join_mask[r], join_mask[r], joined[r], ALU.mult).then_inc(chain.sem, 1))
                    chain.did(dve.tensor_tensor(carried[r], last_prev[r], first[r], ALU.is_equal).then_inc(chain.sem, 1))
                    k = chain.did(dve.tensor_tensor(ends_here[r], first[r], first_next[r], ALU.not_equal).then_inc(chain.sem, 1))
                    dve.wait_ge(chain.sem, chain.after(k))
                    k = chain.did(dve.tensor_tensor(carried[r], carried[r], ends_here[r], ALU.mult).then_inc(chain.sem, 1))
                    dve.wait_ge(chain.sem, chain.after(k))
                    k = chain.did(dve.tensor_scalar(carried[r], carried[r], -SKIP, SKIP, ALU.mult, ALU.add).then_inc(chain.sem, 1))
                    dve.wait_ge(chain.sem, chain.after(k))
                    chain.did(dve.tensor_tensor(join_idx[r], carried[r], first[r], ALU.add).then_inc(chain.sem, 1))
                    for k in range(2):
                        dve.wait_ge(scattered[k].sem, scattered[k].after(1))
                    for name, part, factor in SCALES:
                        k = chain.did(dve.tensor_scalar(W(name, part), W(name, part), factor, None, ALU.mult).then_inc(chain.sem, 1))
                    dve.wait_ge(chain.sem, chain.after(k))
                    for k, name in enumerate(("rw1", "rw2")):
                        m = mean[0:65, k:k + 1]
                        k = chain.did(dve.tensor_reduce(m, W(name), AX_X, ALU.add).then_inc(chain.sem, 1))
                        dve.wait_ge(chain.sem, chain.after(k))
                        k = chain.did(dve.tensor_scalar(m, m, 1.0 / 64, None, ALU.mult).then_inc(chain.sem, 1))
                        dve.wait_ge(chain.sem, chain.after(k))
                        chain.did(dve.tensor_scalar(W(name), W(name), m, None, ALU.subtract).then_inc(chain.sem, 1))
                    for k, (norm, weights) in enumerate(folds):
                        dve.wait_ge(setup_mm.sem, setup_mm.after(k + 1))
                        chain.did(dve.scalar_tensor_tensor(W(weights), W(weights), W(norm, cols=(65, 66)), bank(k, 65, 128),
                                                     ALU.mult, ALU.add).then_inc(chain.sem, 1))
                    for norm, weights in (("ln1_v", "sd_v"), ("ln2_v", "f1_v")):
                        chain.did(dve.tensor_scalar(W(weights), W(weights), W(norm), None, ALU.mult).then_inc(chain.sem, 1))
                    dve.wait_ge(setup_step.sem, setup_step.after(chain.n))

            for sig in scattered:
                sig.passed(1)

        with nc.Block() as block:
            @block.vector
            def _(dve):
                for sig in signals:
                    if sig.credit:
                        dve.sem_inc(sig.sem, sig.credit * sig.unit)
        setup()
        node_pre()
        edge_logits()
        edge_softmax()
        join(0)
        node_first()
        for layer in (1, 2, 3):
            edge_layer(layer)
            join(layer)
            node_layer(layer)


def kernel(**inputs):
    import concourse.bacc as _bacc
    from concourse.bass_utils import run_bass_kernel_spmd as _run

    n = inputs["x"].shape[0]
    arrays = layout(inputs)
    nc = _bacc.Bacc("TRN2", target_bir_lowering=False, num_devices=1)
    inp = {name: nc.dram_tensor(f"in_{name}", a.shape, mybir.dt.from_np(a.dtype), kind="ExternalInput").ap()
           for name, a in arrays.items()}
    nodes = arrays["x"].shape[0]
    out = nc.dram_tensor("out", (nodes, ROW), F32, kind="ExternalOutput").ap()
    gnn_kernel(nc, inp, out)
    r = _run(nc, [{f"in_{name}": a for name, a in arrays.items()}], core_ids=[0])
    return r.results[0]["out"][:n, :D]


def layout(inputs):
    i = {k: np.asarray(v) for k, v in inputs.items()}
    n = i["x"].shape[0]
    nodes = -(-n // (2 * CHUNK)) * 2 * CHUNK
    chunks, tiles = nodes // CHUNK, nodes // P

    def rows(a, fill=0):
        return np.concatenate([a, np.full((nodes - n,) + a.shape[1:], fill, a.dtype)])

    src, dst = rows(i["src"]), rows(i["dst"], n)
    by_tile = [a.reshape(chunks, TILES, P).transpose(0, 2, 1) for a in (src, dst)]
    follow = np.append(dst[1:], np.int32(nodes))
    before = np.append(np.int32(-1), dst[:-1])
    tail = np.zeros(P - 1, dst.dtype)
    blocks = (FIX_BLOCKS, tiles // FIX_BLOCKS)
    first, last = dst[::P], dst[P - 1::P]
    vec, sh = rows(i["edge_attr_3"]), rows(i["edge_attr_4"])
    ones = np.ones((nodes, 1), np.float32)
    t = np.arange(tiles)
    triangle = (t[:, None] < t[None, :]).astype(np.float32)
    arrays = {
        "x": np.concatenate([rows(i["x"]), rows(i["node_vec1"])], 1),
        "edge_idx": np.concatenate(by_tile, 2),
        "dst_flat": dst[None],
        "dst_cols": dst.reshape(tiles, P).T,
        "dst_cols_next": follow.reshape(tiles, P).T,
        "dst_prev": np.concatenate([before, dst[-1:], tail]).reshape(P, tiles + 1),
        "dst_cur": np.concatenate([dst, follow[-1:], tail]).reshape(P, tiles + 1),
        "tile_first": first.reshape(blocks).T,
        "tile_first_next": np.append(first[1:], np.int32(nodes)).reshape(blocks).T,
        "tile_last": last.reshape(blocks).T,
        "tile_last_prev": np.append(np.int32(-1), last[:-1]).reshape(blocks).T,
        "tile_first_row": first[None],
        "triangle": triangle.reshape(*blocks, tiles).transpose(1, 0, 2),
        "attr4": np.concatenate([sh, sh[:, 1:3]], 1),
        "vec": np.concatenate([ones, vec, vec[:, 0:2]], 1),
        "scal_1": rows(i["edge_attr_16"]).T,
        "scal_2": rows(i["edge_attr_8"]).T,
        "scal_3": np.concatenate([rows(i["edge_attr_64"]), ones], 1).T,
        "weights": pack_weights(i),
    }
    return {k: np.ascontiguousarray(a) for k, a in arrays.items()}


def pack_weights(i):
    f = np.float32

    def xv(w):
        u, c = w.shape
        m = np.zeros((u, 3, 3, c), f)
        for k in range(3):
            m[:, k, k, :] = w
        return m.reshape(3 * u, 3 * c)

    def xv_mixed(w):
        u, c = w.shape
        m = np.zeros((u, 3, c, 3), f)
        for k in range(3):
            m[:, k, :, k] = w
        return m.reshape(3 * u, 3 * c)

    def below(w, b):
        return np.concatenate([w, np.reshape(b, (1, -1))], 0)

    def norm(w, b):
        m = np.zeros((65, 66), f)
        m[0:64, 64], m[0:64, 65], m[64, 65] = b, w, 1
        return m

    def twice(w):
        r, c = w.shape
        m = np.zeros((2, r, 2, c), f)
        m[0, :, 0], m[1, :, 1] = w, w
        return m.reshape(2 * r, 2 * c)

    def every(w):
        return np.broadcast_to(w, (P, w.shape[-1]))

    L0 = {k[7:]: v for k, v in i.items() if k.startswith("L0_gnn_")}
    heads = np.zeros((HEADS, 8, HEADS), f)
    for h in range(HEADS):
        heads[h, :, h] = L0["alpha_dot"][h]
    post_1 = np.zeros((97, 66), f)
    post_1[0:96, 0:64], post_1[0:96, 64:65], post_1[96, 65] = i["L1_gnn_Wl2_s"], i["L1_gnn_Wa"], 1
    w = {
        "ident": np.eye(P, dtype=f), "ones": np.ones((P, 512), f),
        "ln1_s": norm(L0["ln1_w0"], L0["ln1_b0"]), "ln1_v": np.repeat(L0["ln1_w1"], 3)[:, None],
        "ln2_s": norm(L0["ln2_w0"], L0["ln2_b0"]), "ln2_v": np.repeat(L0["ln2_w1"], 3)[:, None],
        "sd_s": np.concatenate([below(L0["msrc_ws"], np.zeros(64, f)), below(L0["mdst_ws"], L0["mdst_bs"])], 1),
        "sd_v": np.concatenate([xv(L0["msrc_wv"]), xv(L0["mdst_wv"])], 1),
        "rw1": below(L0["rw1"], L0["rb1"]), "rg1": every(L0["rg1"]), "rbe1": every(L0["rbe1"]),
        "rw2": below(L0["rw2"], L0["rb2"]), "rg2": every(L0["rg2"]), "rbe2": every(L0["rbe2"]),
        "rw3": below(L0["rw3"], L0["roff"]),
        "lin_s": below(L0["lin_ws"], L0["lin_bs"]), "lin_v": L0["lin_wv"], "adot": heads.reshape(64, HEADS),
        "proj_s": below(L0["proj_ws"], L0["proj_bs"]), "proj_v": xv_mixed(L0["proj_wv"]),
        "f1_s": below(L0["f1_ws"], L0["f1_bs"])[:, 0:128],
        "f1_g": np.tile(below(L0["f1_ws"], L0["f1_bs"])[:, 128:192], (1, 2)),
        "f1_v": xv(L0["f1_wv"]),
        "f2_s": L0["f2_ws"], "f2_b": L0["f2_bs"][None], "f2_v": twice(L0["f2_wv"]),
        "e_s1": i["L1_gnn_Wl1_0"], "e_v1": xv(i["L1_gnn_Wl1_1"]), "fc1_1": i["L1_gnn_Wfc1"], "fc2_1": i["L1_gnn_Wfc2"],
        "post_s1": post_1, "post_v1": i["L1_gnn_Wl2_v"], "sc_s1": i["L1_gnn_Wsc0"], "sc_v1": xv_mixed(i["L1_gnn_Wsc1"]),
        "e_s2": i["L2_gnn_lin1_w0"], "e_v2": xv(i["L2_gnn_lin1_w1"]), "fc1_2": i["L2_gnn_fc_w1"], "fc2_2": i["L2_gnn_fc_w2"],
        "post_s2": np.concatenate([i["L2_gnn_lin2_w0"], i["L2_gnn_lin3_w"]], 1), "post_v2": i["L2_gnn_lin2_w1"],
        "sc_s2": i["L2_gnn_sc_w0"], "sc_v2": xv_mixed(i["L2_gnn_sc_w1"]),
        "e_s3": i["L3_gnn_lin1_ws"], "e_v3": xv(i["L3_gnn_lin1_wv"]), "fc1_3": i["L3_gnn_fc_w1"], "fc2_3": i["L3_gnn_fc_w2"],
        "post_s3": i["L3_gnn_lin2_ws"], "post_v3": i["L3_gnn_lin2_wv"],
        "sc_s3": i["L3_gnn_sc_ws"], "sc_v3": xv_mixed(i["L3_gnn_sc_wv"]),
    }
    out = np.zeros((P, WCOLS), f)
    for name, (r, c) in SHAPES.items():
        out[0:r, OFFSETS[name]:OFFSETS[name] + c] = np.reshape(w[name], (r, c))
    return out
```
